# Optimizing a Trainium2 kernel written in Bass

```python
import numpy as np
import jax
import jax.numpy as jnp

def _softmax(x, axis=-1):
    return jax.nn.softmax(x, axis=axis)

def _gelu(x):
    return jax.nn.gelu(x, approximate=True)

def _silu(x):
    return jax.nn.silu(x)

def _sigmoid(x):
    return jax.nn.sigmoid(x)

def _layernorm(x, axis=-1, eps=1e-05):
    m = jnp.mean(x, axis=axis, keepdims=True)
    v = jnp.var(x, axis=axis, keepdims=True)
    return (x - m) / jnp.sqrt(v + eps)

def _scatter_add(tgt, idx, src, axis=0):
    return tgt.at[idx].add(src)

def _segment_sum(src, seg, n):
    return jax.ops.segment_sum(src, seg, n)
kernel_name = 'mk_adj_ffn_d1_adj_r2_e019e5'

def setup_inputs(seed: int=0):
    np.random.seed(seed)
    _w = jnp.asarray

    def _rec_inputs():
        import jax
        import jax.numpy as jnp
        _gk = jax.random.key(seed)
        x = -0.0005207 + 1.001 * jax.random.normal(jax.random.fold_in(_gk, 1), (8192, 128), jnp.float32)
        _a = jax.random.bernoulli(jax.random.fold_in(_gk, 2), 0.000488281, (8192, 8192))
        _a = jnp.logical_or(_a, jnp.swapaxes(_a, -1, -2))
        _a = jnp.logical_or(_a, jnp.eye(8192, dtype=bool))
        _af = _a.astype(jnp.float32)
        _af = _af * jax.random.uniform(jax.random.fold_in(_gk, 3), (8192, 8192), jnp.float32, 0.05, 1)
        adj = _af
        return (x, adj)
    x, adj = _rec_inputs()

    def _L0_gnn_setup():
        import jax, jax.numpy as jnp
        import numpy as np
        N = 4096
        F_IN = 128
        F_OUT = 128
        key = jax.random.key(seed)
        k1, k2, k3 = jax.random.split(key, 3)
        H = jax.random.normal(k1, (N, F_IN), dtype=jnp.float32)
        A_tilde = jax.random.uniform(k2, (N, N), dtype=jnp.float32)
        limit = np.sqrt(6.0 / (F_IN + F_OUT)).astype(np.float32)
        W = jax.random.uniform(k3, (F_IN, F_OUT), dtype=jnp.float32, minval=-limit, maxval=limit)
        return {'H': H, 'A_tilde': A_tilde, 'W': W}
    _L0_gnn_all = _L0_gnn_setup()
    _L0_gnn_in = {k: v for k, v in _L0_gnn_all.items() if k in ('W',)}
    del _L0_gnn_all

    def _L0_ffn_setup():
        import jax, jax.numpy as jnp
        import numpy as np
        B, K, D = (256, 16, 128)
        E = 32
        H = int(D * 0.25)
        key = jax.random.key(seed)
        ks = jax.random.split(key, 7)
        d_rs = D ** (-0.5)
        h_rs = H ** (-0.5)
        x = jax.random.normal(ks[0], (B, K, D), dtype=jnp.float32)
        router_w = jax.random.uniform(ks[1], (E, D), jnp.float32, -d_rs, d_rs)
        router_b = jax.random.uniform(ks[2], (E,), jnp.float32, -d_rs, d_rs)
        W1 = jax.random.uniform(ks[3], (E, D, H), jnp.float32, -h_rs, h_rs)
        b1 = jax.random.uniform(ks[4], (E, H), jnp.float32, -h_rs, h_rs)
        W2 = jax.random.uniform(ks[5], (E, H, D), jnp.float32, -d_rs, d_rs)
        b2 = jax.random.uniform(ks[6], (E, D), jnp.float32, -d_rs, d_rs)
        return {'x': x, 'router_w': router_w, 'router_b': router_b, 'W1': W1, 'b1': b1, 'W2': W2, 'b2': b2}
    _L0_ffn_all = _L0_ffn_setup()
    _L0_ffn_in = {k: v for k, v in _L0_ffn_all.items() if k in ('router_w', 'router_b', 'W1', 'b1', 'W2', 'b2')}
    del _L0_ffn_all
    return {'x': x, 'adj': adj, 'L0_gnn_W': _L0_gnn_in['W'], 'L0_ffn_router_w': _L0_ffn_in['router_w'], 'L0_ffn_router_b': _L0_ffn_in['router_b'], 'L0_ffn_W1': _L0_ffn_in['W1'], 'L0_ffn_b1': _L0_ffn_in['b1'], 'L0_ffn_W2': _L0_ffn_in['W2'], 'L0_ffn_b2': _L0_ffn_in['b2']}

def reference(x, adj, L0_gnn_W, L0_ffn_router_w, L0_ffn_router_b, L0_ffn_W1, L0_ffn_b1, L0_ffn_W2, L0_ffn_b2):
    import jax
    import jax.numpy as jnp

    def _L0_gnn_ref(H, A_tilde, W):
        import jax, jax.numpy as jnp
        import numpy as np
        N = 4096
        F_IN = 128
        F_OUT = 128
        d_inv_sqrt = jnp.sum(A_tilde, axis=1) ** (-0.5)
        A_norm = d_inv_sqrt[:, None] * A_tilde * d_inv_sqrt[None, :]
        H_next = A_norm @ H @ W
        return jax.nn.relu(H_next)

    def _L0_ffn_ref(x, router_w, router_b, W1, b1, W2, b2):
        import jax, jax.numpy as jnp
        import numpy as np
        B, K, D = (256, 16, 128)
        E = 32
        H = int(D * 0.25)
        xf = x.reshape(-1, D)
        logits = xf @ router_w.T + router_b
        idx = jnp.argmax(logits, axis=-1)
        w1t = jnp.take(W1, idx, axis=0)
        h = jnp.einsum('nd,ndh->nh', xf, w1t) + jnp.take(b1, idx, axis=0)
        h = jax.nn.relu(h)
        w2t = jnp.take(W2, idx, axis=0)
        out = jnp.einsum('nh,nhd->nd', h, w2t) + jnp.take(b2, idx, axis=0)
        out = jax.nn.relu(out)
        return out.reshape(x.shape)
    x = x + _L0_gnn_ref(_layernorm(x, axis=-1), adj, L0_gnn_W)
    x = x + _L0_ffn_ref(_layernorm(x, axis=-1)[None], L0_ffn_router_w, L0_ffn_router_b, L0_ffn_W1, L0_ffn_b1, L0_ffn_W2, L0_ffn_b2)[0]
    return x

_drawn_inputs = setup_inputs


def setup_inputs(seed=0):
    import zlib

    import numpy as np

    out = dict(_drawn_inputs(seed))
    spreads = {}
    factors = {'L0_ffn_b1': 4.286}
    for name, (base, spread) in spreads.items():
        noise = np.random.default_rng([zlib.crc32(name.encode()), seed]).standard_normal(out[name].shape)
        drawn = base * np.exp(spread * noise) if base else spread * noise
        out[name] = jnp.asarray(drawn.astype(out[name].dtype))
    for name, factor in factors.items():
        out[name] = (out[name] * factor).astype(out[name].dtype)
    return out
```

```python
from contextlib import ExitStack

import concourse.bass as bass
from concourse import mybir


def gnn_ffn_kernel(nc, x, adj, gnn_w, router_w, router_b, w1, b1, w2, b2, out):
    F32, BF16 = mybir.dt.float32, mybir.dt.bfloat16
    ALU, ACT, AX = mybir.AluOpType, mybir.ActivationFunctionType, mybir.AxisListType

    N, D = x.shape
    E, _, HID = w1.shape
    P = 128
    SQ = 32
    A = B = P // SQ
    ROWS = A * B * SQ
    STRIPS = N // ROWS
    TQ = 4
    QS = STRIPS // TQ
    CW = TQ * B * SQ
    G = A * B
    HG = G // 2
    AHEAD = 1
    EC = P // HID
    SLICES = E // EC
    EPS = 1e-5
    BIG = 1e30

    RAW = 3
    SLOTS = 7
    BANKS = 4
    ACT_GROUPS = 5
    LOOK = 4
    LATE = 3

    halves1 = [(s, q, h) for s in range(STRIPS) for q in reversed(range(QS)) for h in range(2)]
    order2 = [s for s in reversed(range(STRIPS)) if s + AHEAD + 1 < STRIPS]
    halves2 = [(s, q, h) for s in order2 for q in range((s + AHEAD + 1) // TQ, QS) for h in range(2)]
    halves = halves1 + halves2

    def blocks_of(n):
        s, q, _ = halves[n]
        if n < len(halves1):
            return [t for t in range(TQ * q, TQ * q + TQ) if t <= s + AHEAD]
        return [t for t in range(TQ * q, TQ * q + TQ) if t > s + AHEAD]

    transposed = [(s, t) for n, (s, q, h) in enumerate(halves) if h == 1 for t in blocks_of(n)]
    left = {s: [(r, t) for r, t in transposed if r == s and t < s] for s in range(STRIPS)}
    column = {s: [(r, s) for r in range(max(0, s - AHEAD), s + 1)] for s in range(STRIPS)}
    phase2 = [(s, t) for n, (s, q, h) in enumerate(halves) if n >= len(halves1) and h == 1
              for t in blocks_of(n)]
    product = [blk for s in range(STRIPS) for blk in left[s] + column[s]] + phase2
    N1 = len(product) - len(phase2)
    place = {blk: i for i, blk in enumerate(product)}
    landed = {blk: i for i, blk in enumerate(transposed)}
    slot_of, slot_free = {}, {}
    last = [-1] * SLOTS
    for blk in transposed:
        k = last.index(min(last))
        slot_of[blk], slot_free[blk] = k, last[k] + 1
        last[k] = place[blk]

    opens, closes = set(), {}
    for part in (product[:N1], phase2):
        seen = {}
        for s, t in part:
            seen.setdefault(s, []).append((s, t))
        for s, blks in seen.items():
            opens.add(blks[0])
            closes[blks[-1]] = s
    closing = [blk for blk in product if blk in closes]
    closed_by = {blk: i + 1 for i, blk in enumerate(closing)}
    done_1 = {closes[blk]: place[blk] + 1 for blk in closing if place[blk] < N1}

    ffn = [s for s in range(STRIPS) if s not in order2] + order2
    start = [round((len(phase2) - 1) * n / (STRIPS - 1)) for n in range(STRIPS)]
    STEP = (0, 2, 3, 4, 5)
    for n, s in enumerate(ffn):
        assert s not in order2 or start[n] >= place[[b for b in phase2 if b[0] == s][-1]] - N1
    steps_at = {}
    for n in range(STRIPS):
        if n:
            steps_at.setdefault(start[n], []).append(("emit", n - 1))
        for k, d in enumerate(STEP):
            steps_at.setdefault(start[n] + d, []).append((("message", "flip", "route", "choose", "experts")[k], n))
    steps_at.setdefault(start[-1] + STEP[-1] + 1, []).append(("emit", STRIPS - 1))
    TAIL = start[-1] + STEP[-1] + 2

    adj_v = adj.rearrange("(q a t b r) c -> q t r a b c", q=QS, a=A, t=TQ, b=B, r=SQ)
    x_v = x.rearrange("(q a t b r) f -> q t a r b f", q=QS, a=A, t=TQ, b=B, r=SQ)
    out_v = out.rearrange("(q a t b r) f -> q t a r b f", q=QS, a=A, t=TQ, b=B, r=SQ)

    ctx = ExitStack()
    with ctx:
        def sb(name, shape, dt=F32):
            return ctx.enter_context(nc.sbuf_tensor(name, shape, dt))

        def sem(name):
            return ctx.enter_context(nc.semaphore(name))

        raw = sb("raw", [P, RAW, HG, CW])
        turned = sb("turned", [P, SLOTS, B, ROWS])
        g = sb("g", [P, STRIPS, B, D])
        prod = sb("prod", [P, STRIPS, ROWS])
        rowscale = sb("rowscale", [P, STRIPS, B])
        root = sb("root", [P, B])
        part = sb("part", [P, 2, G, QS])
        part_q = sb("part_q", [P, G])
        ident = sb("ident", [P, P])
        quads = sb("quads", [P, A, SQ])
        eps = sb("eps", [P, 1])
        w_sb = sb("w_sb", [P, D])
        rw_nat = sb("rw_nat", [E, D])
        rw_t = sb("rw_t", [P, E])
        rb = sb("rb", [P, E])
        w1_sb = sb("w1_sb", [P, E, HID])
        b1_nat = sb("b1_nat", [SLICES, P])
        b1_t = sb("b1_t", [P, SLICES])
        w2_sb = sb("w2_sb", [P, SLICES, D])
        b2_sb = sb("b2_sb", [E, D])
        off = sb("off", [E, E, HID], BF16)
        count = sb("count", [P, B, E])
        xs = sb("xs", [P, 2, B, D])
        stats = sb("stats", [P, B, 6])
        mv = sb("mv", [P, B, 2])
        rstd = sb("rstd", [P, 2, B])
        x1 = sb("x1", [P, 2, B, D])
        y = sb("y", [P, B, D])
        y_t = sb("y_t", [P, B * P])
        logit = sb("logit", [P, B, E])
        best = sb("best", [P, B])
        hit = sb("hit", [P, B, E])
        first = sb("first", [P, B])
        onehot = sb("onehot", [P, B, E])
        hot_f = sb("hot_f", [E, B * P])
        hot_b = sb("hot_b", [E, B * P], BF16)
        hid = sb("hid", [P, 2, B * P])

        banks = [ctx.enter_context(nc.psum_tensor(f"bank{i}", [P, 512], F32)) for i in range(8)]
        open_ = banks[:BANKS]
        pz = banks[4:6]
        po = banks[6]
        pm = banks[7]

        raw_in = [sem(f"raw_in{i}") for i in range(RAW)]
        raw_by_dve = sem("raw_by_dve")
        raw_by_act = sem("raw_by_act")
        block_turned = sem("block_turned")
        block_used = sem("block_used")
        prod_saved = sem("prod_saved")
        const_pool = sem("const_pool")
        const_dma = sem("const_dma")
        const_turned = sem("const_turned")
        const_kept = sem("const_kept")
        x_in = [sem(f"x_in{i}") for i in range(2)]
        norm_var = sem("norm_var")
        norm_root = sem("norm_root")
        ln_ready = sem("ln_ready")
        ln_turned = sem("ln_turned")
        ln_t_kept = sem("ln_t_kept")
        xw_ready = sem("xw_ready")
        sums_part = sem("sums_part")
        sums_full = sem("sums_full")
        sums_root = sem("sums_root")
        g_ready = sem("g_ready")
        dve_chain = sem("dve_chain")
        f_prod_turned = sem("f_prod_turned")
        f_msg = sem("f_msg")
        f_y = sem("f_y")
        f_y_turned = sem("f_y_turned")
        f_y_t = sem("f_y_t")
        f_logits = sem("f_logits")
        f_onehot = sem("f_onehot")
        f_hot_turned = sem("f_hot_turned")
        f_hot = sem("f_hot")
        f_z = sem("f_z")
        f_hid = sem("f_hid")
        f_o_part = sem("f_o_part")
        f_ffn_t = sem("f_ffn_t")
        f_out_turned = sem("f_out_turned")
        f_res = sem("f_res")
        stored = [sem(f"stored{i}") for i in range(2)]

        def as_read(bank):
            return bank[:, :].rearrange("p (a b r) -> p a b r", a=A, b=B)

        def by_share(v):
            return v.rearrange("p (b a r) -> p a b r", a=A, b=B)

        CONST_DMAS = 7
        HALF_IN = 16 * A * (HG // B)
        block = ctx.enter_context(nc.Block())

        @block.sync
        def _(sp):
            for n, (s, q, h) in enumerate(halves):
                if n >= RAW:
                    m = n - RAW
                    if m < len(halves1) or halves[m][2] == 0:
                        sp.wait_ge(raw_by_dve, sum(k < len(halves1) or halves[k][2] == 0 for k in range(m + 1)))
                    else:
                        sp.wait_ge(block_turned, landed[(halves[m][0], blocks_of(m)[-1])] + 1)
                    if n - RAW < len(halves1):
                        sp.wait_ge(raw_by_act, ACT_GROUPS * (n - RAW + 1))
                c0 = (blocks_of(n)[0] - TQ * q) * P if n >= len(halves1) else 0
                for a in range(A):
                    col = A * CW * q + CW * a
                    for i in range(HG // B):
                        sp.dma_start(raw[SQ * a:SQ * a + SQ, n % RAW, B * i:B * i + B, c0:CW],
                                     adj_v[s // TQ, s % TQ, :, HG // B * h + i, :, col + c0:col + CW])\
                            .then_inc(raw_in[n % RAW], 16)

        @block.gpsimd
        def _(pool):
            pool.memset(ident[:, :], 0.0).then_inc(const_pool, 1)
            pool.memset(quads[:, :, :], 0.0).then_inc(const_pool, 1)
            pool.memset(off[:, :, :], 0.0).then_inc(const_pool, 1)
            pool.memset(eps[:, :], EPS).then_inc(const_pool, 1)
            pool.wait_ge(const_pool, 4)
            pool.iota(count[:, :, :], pattern=[[0, B], [1, E]], base=-E, channel_multiplier=0,
                      allow_small_or_imprecise_dtypes=True).then_inc(const_pool, 1)
            pool.affine_select(out=ident[:, :], in_=ident[:, :], compare_op=ALU.not_equal, fill=1.0, base=0,
                               pattern=[[-1, P]], channel_multiplier=1).then_inc(const_pool, 1)
            pool.affine_select(out=off[:, :, :], in_=off[:, :, :], compare_op=ALU.is_equal, fill=-BIG, base=0,
                               pattern=[[1, E], [0, HID]], channel_multiplier=-1).then_inc(const_pool, 1)
            for a in range(A):
                pool.affine_select(out=quads[:, :, :], in_=quads[:, :, :], compare_op=ALU.not_equal, fill=1.0,
                                   base=-SQ * a, pattern=[[0, A], [-1, SQ]], channel_multiplier=1)\
                    .then_inc(const_pool, 1)
                pool.wait_ge(const_pool, 8 + a)

            def load_x(k, s):
                if 2 <= k < STRIPS + 2:
                    pool.wait_ge(ln_ready, k - 1)
                elif k >= 2:
                    pool.wait_ge(f_y, k - 1 - STRIPS)
                for a in range(A):
                    pool.dma_start(xs[SQ * a:SQ * a + SQ, k % 2, :, :], x_v[s // TQ, s % TQ, a])\
                        .then_inc(x_in[k % 2], 16)

            for s in range(STRIPS):
                load_x(s, s)
            load_x(STRIPS, ffn[0])
            for n in range(STRIPS):
                if n + 1 < STRIPS:
                    load_x(STRIPS + n + 1, ffn[n + 1])
                s = ffn[n]
                pool.wait_ge(f_res, n + 1)
                for a in range(A):
                    pool.dma_start(out_v[s // TQ, s % TQ, a], x1[SQ * a:SQ * a + SQ, n % 2, :, :])\
                        .then_inc(stored[n % 2], 16)
            for i in range(2):
                pool.wait_ge(stored[i], STRIPS // 2 * A * 16)

        @block.scalar
        def _(act):
            act.dma_start(w_sb[:, :], gnn_w).then_inc(const_dma, 16)
            act.dma_start(rw_nat[:, :], router_w).then_inc(const_dma, 16)
            act.dma_start(b1_nat[:, :], b1.rearrange("(c e) h -> c (e h)", e=EC)).then_inc(const_dma, 16)
            act.dma_start(b2_sb[:, :], b2).then_inc(const_dma, 16)
            act.dma_start(rb[:, :], router_b.rearrange("(o e) -> o e", o=1).broadcast_to((P, E)))\
                .then_inc(const_dma, 16)
            act.dma_start(w1_sb[:, :, :], w1.rearrange("e d h -> d e h")).then_inc(const_dma, 16)
            act.dma_start(w2_sb[:, :, :], w2.rearrange("(c e) h d -> (e h) c d", e=EC)).then_inc(const_dma, 16)
            act.wait_ge(const_turned, 1)
            nc.scalar.activation(rw_t[:, :], pm[:, 0:E], ACT.Copy)
            nc.scalar.activation(b1_t[:, :], pm[:, E:E + SLICES], ACT.Copy).then_inc(const_kept, 1)
            act.wait_ge(const_pool, 4)

            def norm_root_(k):
                act.wait_ge(norm_var, k + 1)
                if k >= 2:
                    act.wait_ge(ln_ready if k <= STRIPS else f_y,
                                k - 1 if k <= STRIPS else k - 1 - STRIPS)
                nc.scalar.activation(rstd[:, k % 2, :], mv[:, :, 1], ACT.Sqrt, bias=eps[:, 0:1])\
                    .then_inc(norm_root, 1)

            def turned_ln(s):
                act.wait_ge(ln_turned, s + 1)
                if s >= 1:
                    act.wait_ge(xw_ready, s)
                nc.scalar.activation(y_t[:, :], pz[0][:, :], ACT.Copy).then_inc(ln_t_kept, 1)

            def save(s):
                act.wait_ge(block_used, done_1[s])
                nc.scalar.activation(by_share(prod[:, s, :]), as_read(open_[s % BANKS]), ACT.Copy).then_inc(prod_saved, 1)

            discard = [hid[:, 0, :], hid[:, 1, :]] + [x1[:, i, :, :].rearrange("p b f -> p (b f)") for i in range(2)]
            norm_root_(0)
            for n, (s, q, h) in enumerate(halves1):
                act.wait_ge(raw_in[n % RAW], HALF_IN * (n // RAW + 1))
                if h == 0 and q == QS - 1 and s >= 2:
                    act.wait_ge(sums_part, s - 1)
                for i in range(ACT_GROUPS):
                    k = ACT_GROUPS * n + i
                    if k >= 4:
                        act.wait_ge(raw_by_act, k - 3)
                    nc.scalar.activation(discard[k % 4], raw[:, n % RAW, i, :], ACT.Copy,
                                         accum_out=part[:, s % 2, HG * h + i, q:q + 1]).then_inc(raw_by_act, 1)
                if h == 1 and q == QS - 1:
                    turned_ln(s)
                    if s + 1 < STRIPS:
                        norm_root_(s + 1)
                    if s >= AHEAD + 1:
                        save(s - AHEAD - 1)
            
                if h == 1 and q == 0:
                    act.wait_ge(sums_full, s + 1)
                    for a in range(A):
                        ins = nc.scalar.activation(root[SQ * a:SQ * a + SQ, :],
                                                   po[SQ * a:SQ * a + SQ, B * a:B * a + B], ACT.Sqrt)
                    ins.then_inc(sums_root, 1)
            for s in range(STRIPS - AHEAD - 1, STRIPS):
                save(s)
            act.wait_ge(raw_by_act, ACT_GROUPS * len(halves1))

            def message(n):
                s = ffn[n]
                act.wait_ge(f_prod_turned, n + 1)
                if n >= 2:
                    act.wait_ge(stored[n % 2], n // 2 * A * 16)
                for b in range(B):
                    ins = nc.scalar.activation(x1[:, n % 2, b, :], pm[:, b * D:b * D + D], ACT.Relu,
                                               scale=rowscale[:, s, b:b + 1])
                ins.then_inc(f_msg, 1)
                norm_root_(STRIPS + n)

            def flip(n):
                act.wait_ge(f_y_turned, n + 1)
                nc.scalar.activation(y_t[:, :], pm[:, :], ACT.Copy).then_inc(f_y_t, 1)

            def choose(n):
                act.wait_ge(f_hot_turned, n + 1)
                nc.scalar.activation(hot_b[:, :], pm[0:E, :], ACT.Copy)
                nc.scalar.activation(hot_f[:, :], pm[0:E, :], ACT.Copy).then_inc(f_hot, 1)

            def experts(n):
                for c in range(SLICES):
                    k = SLICES * n + c
                    act.wait_ge(f_z, k + 1)
                    if k >= 2:
                        act.wait_ge(f_o_part, k - 1)
                    nc.scalar.activation(hid[:, k % 2, :], pz[k % 2][:, :], ACT.Relu, bias=b1_t[:, c:c + 1])\
                        .then_inc(f_hid, 1)
                act.wait_ge(f_o_part, SLICES * (n + 1))
                nc.scalar.activation(prod[:, ffn[n], :], po[:, :], ACT.Relu).then_inc(f_ffn_t, 1)

            for i in range(TAIL):
                for what, n in steps_at.get(i, []):
                    if what == "message":
                        message(n)
                    elif what == "flip":
                        flip(n)
                    elif what == "choose":
                        choose(n)
                    elif what == "experts":
                        experts(n)

        @block.vector
        def _(dve):
            links = [0]

            def chain(ins):
                links[0] += 1
                ins.then_inc(dve_chain, 1)
                dve.wait_ge(dve_chain, links[0])

            def layer_norm(k, src, done):
                for b in range(B):
                    ins = nc.vector.bn_stats(stats[:, b, :], src[:, b, :])
                chain(ins)
                for b in range(B):
                    ins = nc.vector.bn_aggr(mv[:, b, :], stats[:, b, :])
                ins.then_inc(norm_var, 1)
                dve.wait_ge(norm_root, k + 1)
                chain(nc.vector.reciprocal(rstd[:, k % 2, :], rstd[:, k % 2, :]))
                for b in range(B):
                    ins = nc.vector.tensor_scalar(y[:, b, :], src[:, b, :], mv[:, b, 0:1], rstd[:, k % 2, b:b + 1],
                                                  ALU.subtract, ALU.mult)
                ins.then_inc(done, 1)

            def norm_x(s):
                dve.wait_ge(x_in[s % 2], 64 * (s // 2 + 1))
                if s >= 1:
                    dve.wait_ge(ln_turned, s)
                layer_norm(s, xs[:, s % 2, :, :], ln_ready)

            def turn(n, t):
                s, q, h = halves[n]
                blk = (s, t)
                if h == 0 and slot_free[blk] > 0:
                    dve.wait_ge(block_used, slot_free[blk])
                c0 = (t - TQ * q) * P
                src = raw[:, n % RAW, :, c0:c0 + P].rearrange("p g (b c) -> p g b c", c=SQ)
                dst = turned[:, slot_of[blk], :, :].rearrange("p b (g r) -> p g b r", r=SQ)
                ins = nc.vector.transpose(dst[:, HG * h:HG * h + HG, :, :], src)
                if h == 1:
                    ins.then_inc(block_turned, 1)
                return ins

            def finish_sums(s):
                dve.wait_ge(sums_root, s + 1)
                chain(nc.vector.reciprocal(rowscale[:, s, :], root[:, :]))
                dve.wait_ge(xw_ready, s + 1)
                nc.vector.tensor_tensor(g[:, s, :, :], pz[1][:, :].rearrange("p (b f) -> p b f", b=B),
                                        rowscale[:, s, :].unsqueeze(2).broadcast_to((P, B, D)),
                                        ALU.mult).then_inc(g_ready, 1)

            norm_x(0)
            for n, (s, q, h) in enumerate(halves1):
                dve.wait_ge(raw_in[n % RAW], HALF_IN * (n // RAW + 1))
                for t in blocks_of(n):
                    turn(n, t)
                g0 = HG * h + ACT_GROUPS
                nc.vector.tensor_reduce(part[:, s % 2, g0:HG * h + HG, q], raw[:, n % RAW, ACT_GROUPS:HG, :],
                                        AX.X, ALU.add).then_inc(raw_by_dve, 1)
                if h == 1 and q == 0:
                    dve.wait_ge(raw_by_dve, n + 1)
                    dve.wait_ge(raw_by_act, ACT_GROUPS * (n + 1))
                    if s >= 1:
                        dve.wait_ge(sums_full, s)
                    nc.vector.tensor_reduce(part_q[:, :], part[:, s % 2, :, :], AX.X, ALU.add)\
                        .then_inc(sums_part, 1)
                    finish_sums(s)
                if h == 1 and q == QS - 1 and s + 1 < STRIPS:
                    norm_x(s + 1)

            def turn_half(n):
                dve.wait_ge(raw_in[n % RAW], HALF_IN * (n // RAW + 1))
                for t in blocks_of(n):
                    ins = turn(n, t)
                if halves[n][2] == 0:
                    ins.then_inc(raw_by_dve, 1)

            def merge(i):
                blk = phase2[i]
                if blk in closed_by:
                    s = blk[0]
                    dve.wait_ge(block_used, place[blk] + 1)
                    dve.wait_ge(prod_saved, STRIPS)
                    nc.vector.tensor_tensor(by_share(prod[:, s, :]), as_read(open_[s % BANKS]),
                                            by_share(prod[:, s, :]), ALU.add)\
                        .then_inc(prod_saved, 1)

            def message(n):
                k = STRIPS + n
                dve.wait_ge(x_in[k % 2], 64 * (k // 2 + 1))
                dve.wait_ge(f_msg, n + 1)
                chain(nc.vector.tensor_tensor(x1[:, n % 2, :, :], xs[:, k % 2, :, :], x1[:, n % 2, :, :], ALU.add))
                if n >= 1:
                    dve.wait_ge(f_y_turned, n)
                layer_norm(k, x1[:, n % 2, :, :], f_y)

            def route(n):
                def wide(v):
                    return v.unsqueeze(2).broadcast_to((P, B, E))
                dve.wait_ge(f_logits, n + 1)
                chain(nc.vector.tensor_tensor(logit[:, :, :], pm[:, 0:B * E].rearrange("p (b e) -> p b e", b=B),
                                              rb[:, :].unsqueeze(1).broadcast_to((P, B, E)), ALU.add))
                chain(nc.vector.tensor_reduce(best[:, :], logit[:, :, :], AX.X, ALU.max))
                chain(nc.vector.tensor_tensor(hit[:, :, :], logit[:, :, :], wide(best[:, :]), ALU.is_equal))
                chain(nc.vector.tensor_tensor(hit[:, :, :], hit[:, :, :], count[:, :, :], ALU.mult))
                chain(nc.vector.tensor_reduce(first[:, :], hit[:, :, :], AX.X, ALU.min))
                if n >= 1:
                    dve.wait_ge(f_hot_turned, n)
                nc.vector.tensor_tensor(onehot[:, :, :], count[:, :, :], wide(first[:, :]), ALU.is_equal)\
                    .then_inc(f_onehot, 1)

            def emit(n):
                dve.wait_ge(f_out_turned, n + 1)
                nc.vector.tensor_tensor(x1[:, n % 2, :, :], pz[0][:, :].rearrange("p (b f) -> p b f", b=B),
                                        x1[:, n % 2, :, :], ALU.add).then_inc(f_res, 1)

            nxt = len(halves1)
            for i in range(TAIL):
                while nxt < len(halves) and landed[(halves[nxt][0], blocks_of(nxt)[0])] - N1 <= i + LOOK - TQ:
                    turn_half(nxt)
                    nxt += 1
                if i < len(phase2):
                    merge(i)
                for what, n in steps_at.get(i, []):
                    if what == "message":
                        message(n)
                    elif what == "route":
                        route(n)
                    elif what == "emit":
                        emit(n)

        @block.tensor
        def _(pe):
            pe.wait_ge(const_pool, 11)
            pe.wait_ge(const_dma, 16 * CONST_DMAS)
            nc.tensor.transpose(pm[:, 0:E], rw_nat[:, :], ident[0:E, 0:E])
            nc.tensor.transpose(pm[:, E:E + SLICES], b1_nat[:, :], ident[0:SLICES, 0:SLICES])\
                .then_inc(const_turned, 1)
            pe.wait_ge(const_kept, 1)

            def multiply(blk):
                s, t = blk
                pe.wait_ge(block_turned, landed[blk] + 1)
                if blk in opens:
                    if place[blk] >= N1:
                        before = [c for c in closing if place[c] < place[blk] and c[0] % BANKS == s % BANKS]
                        pe.wait_ge(prod_saved, closed_by[before[-1]])
                    elif s >= BANKS:
                        pe.wait_ge(prod_saved, s - BANKS + 1)
                for b in range(B):
                    ins = nc.tensor.matmul(open_[s % BANKS][:, :], g[:, t, b, :], turned[:, slot_of[blk], b, :],
                                           start=(b == 0 and blk in opens), stop=(b == B - 1 and blk in closes))
                ins.then_inc(block_used, 1)

            def turn_ln(s):
                pe.wait_ge(ln_ready, s + 1)
                if s >= 1:
                    pe.wait_ge(ln_t_kept, s)
                for b in range(B):
                    ins = nc.tensor.transpose(pz[0][:, b * P:b * P + P], y[:, b, :], ident[:, :])
                ins.then_inc(ln_turned, 1)

            def times_w(s):
                pe.wait_ge(ln_t_kept, s + 1)
                if s >= 1:
                    pe.wait_ge(g_ready, s)
                for b in range(B):
                    ins = nc.tensor.matmul(pz[1][:, b * D:b * D + D], y_t[:, b * P:b * P + P], w_sb[:, :],
                                           start=True, stop=True)
                ins.then_inc(xw_ready, 1)

            def sum_quads(s):
                pe.wait_ge(sums_part, s + 1)
                if s >= 1:
                    pe.wait_ge(sums_root, s)
                nc.tensor.matmul(po[:, 0:G], quads[:, :, :], part_q[:, :], start=True, stop=True)\
                    .then_inc(sums_full, 1)

            turn_ln(0)
            for s in range(STRIPS):
                late = max(0, len(left[s]) - LATE)
                for blk in left[s][:late]:
                    multiply(blk)
                times_w(s)
                sum_quads(s)
                for blk in left[s][late:]:
                    multiply(blk)
                pe.wait_ge(g_ready, s + 1)
                for blk in column[s]:
                    multiply(blk)
                if s + 1 < STRIPS:
                    turn_ln(s + 1)

            def message(n):
                s = ffn[n]
                pe.wait_ge(prod_saved, closed_by[max((c for c in closing if closes[c] == s),
                                                     key=lambda c: place[c])])
                if n >= 1:
                    pe.wait_ge(f_hot, n)
                for b in range(B):
                    ins = nc.tensor.transpose(pm[:, b * D:b * D + D], prod[:, s, b * P:b * P + P], ident[:, :])
                ins.then_inc(f_prod_turned, 1)

            def flip(n):
                pe.wait_ge(f_y, n + 1)
                pe.wait_ge(f_msg, n + 1)
                for b in range(B):
                    ins = nc.tensor.transpose(pm[:, b * P:b * P + P], y[:, b, :], ident[:, :])
                ins.then_inc(f_y_turned, 1)

            def route(n):
                pe.wait_ge(f_y_t, n + 1)
                for b in range(B):
                    ins = nc.tensor.matmul(pm[:, b * E:b * E + E], y_t[:, b * P:b * P + P], rw_t[:, :],
                                           start=True, stop=True)
                ins.then_inc(f_logits, 1)

            def choose(n):
                pe.wait_ge(f_onehot, n + 1)
                for b in range(B):
                    ins = nc.tensor.transpose(pm[0:E, b * P:b * P + P], onehot[:, b, :], ident[:, :])
                ins.then_inc(f_hot_turned, 1)

            def experts(n):
                pe.wait_ge(f_hot, n + 1)
                if n >= 1:
                    pe.wait_ge(f_res, n)
                    pe.wait_ge(f_ffn_t, n)

                def hidden(c):
                    k = SLICES * n + c
                    if k >= 2:
                        pe.wait_ge(f_hid, k - 1)
                    nc.tensor.matmul(pz[k % 2][:, :], w1_sb[:, EC * c:EC * c + EC, :], y_t[:, :],
                                     start=True, stop=False)
                    nc.tensor.matmul(pz[k % 2][:, :], off[:, EC * c:EC * c + EC, :], hot_b[:, :],
                                     start=False, stop=True).then_inc(f_z, 1)

                def output(c):
                    k = SLICES * n + c
                    pe.wait_ge(f_hid, k + 1)
                    if c == 0:
                        nc.tensor.matmul(po[:, :], b2_sb[:, :], hot_f[:, :], start=True, stop=False)
                    nc.tensor.matmul(po[:, :], w2_sb[:, c, :], hid[:, k % 2, :], start=False,
                                     stop=(c == SLICES - 1)).then_inc(f_o_part, 1)

                hidden(0)
                for c in range(1, SLICES):
                    hidden(c)
                    output(c - 1)
                output(SLICES - 1)

            def emit(n):
                pe.wait_ge(f_ffn_t, n + 1)
                for b in range(B):
                    ins = nc.tensor.transpose(pz[0][:, b * P:b * P + P], prod[:, ffn[n], b * P:b * P + P], ident[:, :])
                ins.then_inc(f_out_turned, 1)

            for i in range(TAIL):
                if i < len(phase2):
                    multiply(phase2[i])
                for what, n in steps_at.get(i, []):
                    {"message": message, "flip": flip, "route": route, "choose": choose,
                     "experts": experts, "emit": emit}[what](n)


_INS = ["x", "adj", "L0_gnn_W", "L0_ffn_router_w", "L0_ffn_router_b", "L0_ffn_W1", "L0_ffn_b1", "L0_ffn_W2",
        "L0_ffn_b2"]


def kernel(**inputs):
    import numpy as np
    import concourse.bacc as bacc
    from concourse.bass_utils import run_bass_kernel_spmd

    nc = bacc.Bacc("TRN2", target_bir_lowering=False, num_devices=1)
    arrays, args = {}, []
    for name in _INS:
        a = np.ascontiguousarray(inputs[name])
        arrays[f"in_{name}"] = a
        args.append(nc.dram_tensor(f"in_{name}", a.shape, mybir.dt.from_np(a.dtype), kind="ExternalInput").ap())
    shape = arrays["in_x"].shape
    args.append(nc.dram_tensor("out_0", shape, mybir.dt.float32, kind="ExternalOutput").ap())
    gnn_ffn_kernel(nc, *args)
    r = run_bass_kernel_spmd(nc, [arrays], core_ids=[0])
    return r.results[0]["out_0"]
```

```python
from contextlib import ExitStack

import concourse.bass as bass
from concourse import mybir


def gnn_ffn_kernel(nc, x, adj, gnn_w, router_w, router_b, w1, b1, w2, b2, out):
    F32, BF16 = mybir.dt.float32, mybir.dt.bfloat16
    ALU, ACT, AX = mybir.AluOpType, mybir.ActivationFunctionType, mybir.AxisListType

    N, D = x.shape
    E, _, HID = w1.shape
    P = 128
    SQ = 32
    A = B = P // SQ
    G = A * B
    ROWS = G * SQ
    STRIPS = N // ROWS
    TQ = 4
    QS = STRIPS // TQ
    HB = B // 2
    CW = HB * TQ * SQ
    KEEP = 2
    EC = P // HID
    SLICES = E // EC
    EPS = 1e-5
    BIG = 1e30

    RAW = 3
    SLOTS = 20
    SLOTS2 = 14
    BANKS = 4
    ACT_GROUPS = 11
    LOOK = 10
    LATE = 4

    def kept(s, t):
        return t <= s + KEEP

    chunks1 = [(s, q, h) for s in range(STRIPS) for q in reversed(range(QS)) for h in range(2)]
    order2 = [s for s in reversed(range(STRIPS)) if not kept(s, STRIPS - 1)]
    chunks2 = [(s, q, h) for s in order2 for q in range(QS) if not kept(s, TQ * q + TQ - 1) for h in range(2)]
    chunks = chunks1 + chunks2

    def pieces_of(n):
        s, q, h = chunks[n]
        return [(s, t, h) for t in range(TQ * q, TQ * q + TQ) if kept(s, t) == (n < len(chunks1))]

    turned_order = [p for n in range(len(chunks)) for p in pieces_of(n)]
    landed = {p: i for i, p in enumerate(turned_order)}
    left = {s: [p for p in turned_order if p[0] == s and p[1] < s] for s in range(STRIPS)}
    column = {s: [(r, s, h) for r in range(s + 1) if kept(r, s) for h in range(2)] for s in range(STRIPS)}
    phase1 = [p for s in range(STRIPS) for p in left[s] + column[s]]
    phase2 = turned_order[len(phase1):]
    product = phase1 + phase2
    N1 = len(phase1)
    place = {p: i for i, p in enumerate(product)}
    slot_of, slot_free = {}, {}
    last = [-1] * SLOTS
    for i, p in enumerate(turned_order):
        k = min(range(SLOTS if i < N1 else SLOTS2), key=lambda j: last[j])
        slot_of[p], slot_free[p] = k, last[k] + 1
        last[k] = place[p]

    def ends(part):
        found = {}
        for p in part:
            found[p[0]] = (found.get(p[0], (p,))[0], p)
        return found

    opens = {f for part in (phase1, phase2) for f, _ in ends(part).values()}
    done_1 = {s: place[l] + 1 for s, (_, l) in ends(phase1).items()}
    done_2 = {s: place[l] + 1 for s, (_, l) in ends(phase2).items()}
    closes = {l for part in (phase1, phase2) for _, l in ends(part).values()}
    saved_1 = {s: s + 1 for s in range(STRIPS)}
    saved_2 = {s: STRIPS + 1 + i for i, s in enumerate(order2)}

    ffn = [s for s in range(STRIPS) if s not in order2] + order2
    start = [(len(phase2) - 1) * n // (STRIPS - 1) for n in range(STRIPS)]
    STEP = (0, 3, 5, 7, 9)
    for n, s in enumerate(ffn):
        assert s not in order2 or start[n] >= done_2[s] - 1 - N1
    steps_at = {}
    for n in range(STRIPS):
        if n:
            steps_at.setdefault(start[n], []).append(("emit", n - 1))
        for k, d in enumerate(STEP):
            steps_at.setdefault(start[n] + d, []).append((("message", "flip", "route", "choose", "experts")[k], n))
    steps_at.setdefault(start[-1] + STEP[-1] + 1, []).append(("emit", STRIPS - 1))
    TAIL = start[-1] + STEP[-1] + 2

    adj_v = adj.rearrange("(q g t r) c -> q t r g c", q=QS, g=G, t=TQ, r=SQ)
    x_v = x.rearrange("(q a b t r) f -> q t a r b f", q=QS, a=A, b=B, t=TQ, r=SQ)
    out_v = out.rearrange("(q a b t r) f -> q t a r b f", q=QS, a=A, b=B, t=TQ, r=SQ)

    ctx = ExitStack()
    with ctx:
        def sb(name, shape, dt=F32):
            return ctx.enter_context(nc.sbuf_tensor(name, shape, dt))

        def sem(name):
            return ctx.enter_context(nc.semaphore(name))

        raw = sb("raw", [P, RAW, G, CW])
        turned = sb("turned", [P, SLOTS, HB, ROWS])
        g = sb("g", [P, STRIPS, B, D])
        prod = sb("prod", [P, STRIPS, ROWS])
        rowscale = sb("rowscale", [P, STRIPS, B])
        root = sb("root", [P, B])
        part = sb("part", [P, 2, G, 2 * QS])
        part_q = sb("part_q", [P, G])
        ident = sb("ident", [P, P])
        quads = sb("quads", [P, A, SQ])
        eps = sb("eps", [P, 1])
        w_sb = sb("w_sb", [P, D])
        rw_nat = sb("rw_nat", [E, D])
        rw_t = sb("rw_t", [P, E])
        rb = sb("rb", [P, E])
        b1_nat = sb("b1_nat", [SLICES, P])
        b1_t = sb("b1_t", [P, SLICES])
        b2_sb = sb("b2_sb", [E, D])
        off = sb("off", [E, E, HID], BF16)
        count = sb("count", [P, B, E])
        xs = sb("xs", [P, 2, B, D])
        stats = sb("stats", [P, B, 6])
        mv = sb("mv", [P, B, 2])
        rstd = sb("rstd", [P, 2, B])
        y = sb("y", [P, B, D])
        y_t = sb("y_t", [P, B * P])
        best = sb("best", [P, B])
        first = sb("first", [P, B])

        def spare(k, at, size):
            return turned[:, SLOTS2 + k, :, :].rearrange("p b r -> p (b r)")[:, at:at + size]

        w1_sb = spare(0, 0, E * HID).rearrange("p (e h) -> p e h", e=E)
        w2_sb = spare(1, 0, SLICES * D).rearrange("p (c d) -> p c d", c=SLICES)
        hid = spare(2, 0, 2 * B * P).rearrange("p (k r) -> p k r", k=2)
        x1 = spare(3, 0, 2 * B * D).rearrange("p (k b d) -> p k b d", k=2, b=B)
        hot_f = spare(4, 0, B * P)[0:E, :]
        hot_b = spare(4, B * P, B * P // 2).bitcast(BF16)[0:E, :]
        logit, hit, onehot = (spare(5, k * B * E, B * E).rearrange("p (b e) -> p b e", b=B) for k in range(3))

        banks = [ctx.enter_context(nc.psum_tensor(f"bank{i}", [P, 512], F32)) for i in range(8)]
        open_ = banks[:BANKS]
        pz = banks[4:6]
        po = banks[6]
        pm = banks[7]

        raw_in = [sem(f"raw_in{i}") for i in range(RAW)]
        raw_summed = sem("raw_summed")
        raw_by_act = sem("raw_by_act")
        piece_turned = sem("piece_turned")
        piece_used = sem("piece_used")
        prod_saved = sem("prod_saved")
        const_pool = sem("const_pool")
        const_dma = sem("const_dma")
        experts_in = sem("experts_in")
        const_turned = sem("const_turned")
        const_kept = sem("const_kept")
        x_in = [sem(f"x_in{i}") for i in range(2)]
        norm_var = sem("norm_var")
        norm_root = sem("norm_root")
        ln_ready = sem("ln_ready")
        ln_turned = sem("ln_turned")
        ln_t_kept = sem("ln_t_kept")
        xw_ready = sem("xw_ready")
        sums_part = sem("sums_part")
        sums_full = sem("sums_full")
        sums_root = sem("sums_root")
        g_ready = sem("g_ready")
        dve_chain = sem("dve_chain")
        f_prod_turned = sem("f_prod_turned")
        f_msg = sem("f_msg")
        f_y = sem("f_y")
        f_y_turned = sem("f_y_turned")
        f_y_t = sem("f_y_t")
        f_logits = sem("f_logits")
        f_onehot = sem("f_onehot")
        f_hot_turned = sem("f_hot_turned")
        f_hot = sem("f_hot")
        f_z = sem("f_z")
        f_hid = sem("f_hid")
        f_o_part = sem("f_o_part")
        f_ffn_t = sem("f_ffn_t")
        f_out_turned = sem("f_out_turned")
        f_res = sem("f_res")
        stored = [sem(f"stored{i}") for i in range(2)]

        def as_read(bank):
            return bank[:, :].rearrange("p (a b r) -> p a b r", a=A, b=B)

        def by_share(v):
            return v.rearrange("p (b a r) -> p a b r", a=A, b=B)

        CONST_DMAS = 5
        CHUNK_IN = 16 * A
        block = ctx.enter_context(nc.Block())

        @block.sync
        def _(sp):
            for n, (s, q, h) in enumerate(chunks):
                if n >= RAW:
                    m = n - RAW
                    if pieces_of(m):
                        sp.wait_ge(piece_turned, landed[pieces_of(m)[-1]] + 1)
                    else:
                        sp.wait_ge(raw_summed, m + 1)
                    if m < len(chunks1):
                        sp.wait_ge(raw_by_act, ACT_GROUPS * (m + 1))
                for a in range(A):
                    col = (q * A + a) * 2 * CW + h * CW
                    sp.dma_start(raw[SQ * a:SQ * a + SQ, n % RAW, :, :],
                                 adj_v[s // TQ, s % TQ, :, :, col:col + CW]).then_inc(raw_in[n % RAW], 16)

        @block.gpsimd
        def _(pool):
            pool.memset(ident[:, :], 0.0).then_inc(const_pool, 1)
            pool.memset(quads[:, :, :], 0.0).then_inc(const_pool, 1)
            pool.memset(off[:, :, :], 0.0).then_inc(const_pool, 1)
            pool.memset(eps[:, :], EPS).then_inc(const_pool, 1)
            pool.wait_ge(const_pool, 4)
            pool.iota(count[:, :, :], pattern=[[0, B], [1, E]], base=-E, channel_multiplier=0,
                      allow_small_or_imprecise_dtypes=True).then_inc(const_pool, 1)
            pool.affine_select(out=ident[:, :], in_=ident[:, :], compare_op=ALU.not_equal, fill=1.0, base=0,
                               pattern=[[-1, P]], channel_multiplier=1).then_inc(const_pool, 1)
            pool.affine_select(out=off[:, :, :], in_=off[:, :, :], compare_op=ALU.is_equal, fill=-BIG, base=0,
                               pattern=[[1, E], [0, HID]], channel_multiplier=-1).then_inc(const_pool, 1)
            for a in range(A):
                pool.affine_select(out=quads[:, :, :], in_=quads[:, :, :], compare_op=ALU.not_equal, fill=1.0,
                                   base=-SQ * a, pattern=[[0, A], [-1, SQ]], channel_multiplier=1)\
                    .then_inc(const_pool, 1)
                pool.wait_ge(const_pool, 8 + a)

            def load_x(k, s):
                if 2 <= k < STRIPS + 2:
                    pool.wait_ge(ln_turned, k - 1)
                elif k >= 2:
                    pool.wait_ge(f_y, k - 1 - STRIPS)
                for a in range(A):
                    pool.dma_start(xs[SQ * a:SQ * a + SQ, k % 2, :, :], x_v[s // TQ, s % TQ, a])\
                        .then_inc(x_in[k % 2], 16)

            for s in range(STRIPS):
                load_x(s, s)
            load_x(STRIPS, ffn[0])
            pool.wait_ge(piece_used, N1)
            pool.dma_start(w1_sb, w1.rearrange("e d h -> d e h")).then_inc(experts_in, 16)
            pool.dma_start(w2_sb, w2.rearrange("(c e) h d -> (e h) c d", e=EC)).then_inc(experts_in, 16)
            for n in range(STRIPS):
                if n + 1 < STRIPS:
                    load_x(STRIPS + n + 1, ffn[n + 1])
                s = ffn[n]
                pool.wait_ge(f_res, n + 1)
                for a in range(A):
                    pool.dma_start(out_v[s // TQ, s % TQ, a], x1[SQ * a:SQ * a + SQ, n % 2, :, :])\
                        .then_inc(stored[n % 2], 16)
            for i in range(2):
                pool.wait_ge(stored[i], STRIPS // 2 * A * 16)

        @block.scalar
        def _(act):
            act.dma_start(w_sb[:, :], gnn_w).then_inc(const_dma, 16)
            act.dma_start(rw_nat[:, :], router_w).then_inc(const_dma, 16)
            act.dma_start(b1_nat[:, :], b1.rearrange("(c e) h -> c (e h)", e=EC)).then_inc(const_dma, 16)
            act.dma_start(b2_sb[:, :], b2).then_inc(const_dma, 16)
            act.dma_start(rb[:, :], router_b.rearrange("(o e) -> o e", o=1).broadcast_to((P, E)))\
                .then_inc(const_dma, 16)
            act.wait_ge(const_turned, 1)
            nc.scalar.activation(rw_t[:, :], pm[:, 0:E], ACT.Copy)
            nc.scalar.activation(b1_t[:, :], pm[:, E:E + SLICES], ACT.Copy).then_inc(const_kept, 1)
            act.wait_ge(const_pool, 4)

            def norm_root_(k):
                act.wait_ge(norm_var, k + 1)
                if k >= 2:
                    act.wait_ge(ln_ready if k <= STRIPS else f_y,
                                k - 1 if k <= STRIPS else k - 1 - STRIPS)
                nc.scalar.activation(rstd[:, k % 2, :], mv[:, :, 1], ACT.Sqrt, bias=eps[:, 0:1])\
                    .then_inc(norm_root, 1)

            def turned_ln(s):
                act.wait_ge(ln_turned, s + 1)
                if s >= 1:
                    act.wait_ge(xw_ready, s)
                nc.scalar.activation(y_t[:, :], pz[0][:, :], ACT.Copy).then_inc(ln_t_kept, 1)

            def save(s):
                act.wait_ge(piece_used, done_1[s])
                nc.scalar.activation(by_share(prod[:, s, :]), as_read(open_[s % BANKS]), ACT.Copy).then_inc(prod_saved, 1)

            discard = [pm[:, i * CW:i * CW + CW] for i in range(2)]
            act.wait_ge(const_kept, 1)
            norm_root_(0)
            for n, (s, q, h) in enumerate(chunks1):
                act.wait_ge(raw_in[n % RAW], CHUNK_IN * (n // RAW + 1))
                if h == 0 and q == QS - 1 and s >= 2:
                    act.wait_ge(sums_part, s - 1)
                for i in range(ACT_GROUPS):
                    k = ACT_GROUPS * n + i
                    if k >= 2:
                        act.wait_ge(raw_by_act, k - 1)
                    nc.scalar.activation(discard[k % 2], raw[:, n % RAW, i, :], ACT.Copy,
                                         accum_out=part[:, s % 2, i, 2 * q + h:2 * q + h + 1])\
                        .then_inc(raw_by_act, 1)
                if h == 1 and q == QS - 1 and s + 1 < STRIPS:
                    norm_root_(s + 1)
                if h == 0 and q == 1:
                    turned_ln(s)
                    if s >= KEEP + 1:
                        save(s - KEEP - 1)
                if h == 1 and q == 0:
                    act.wait_ge(sums_full, s + 1)
                    for a in range(A):
                        ins = nc.scalar.activation(root[SQ * a:SQ * a + SQ, :],
                                                   po[SQ * a:SQ * a + SQ, B * a:B * a + B], ACT.Sqrt)
                    ins.then_inc(sums_root, 1)
            for s in range(STRIPS - KEEP - 1, STRIPS):
                save(s)

            def message(n):
                s = ffn[n]
                act.wait_ge(f_prod_turned, n + 1)
                if n >= 2:
                    act.wait_ge(stored[n % 2], n // 2 * A * 16)
                for b in range(B):
                    ins = nc.scalar.activation(x1[:, n % 2, b, :], pm[:, b * D:b * D + D], ACT.Relu,
                                               scale=rowscale[:, s, b:b + 1])
                ins.then_inc(f_msg, 1)
                norm_root_(STRIPS + n)

            def flip(n):
                act.wait_ge(f_y_turned, n + 1)
                nc.scalar.activation(y_t[:, :], pm[:, :], ACT.Copy).then_inc(f_y_t, 1)

            def choose(n):
                act.wait_ge(f_hot_turned, n + 1)
                nc.scalar.activation(hot_b[:, :], pm[0:E, :], ACT.Copy)
                nc.scalar.activation(hot_f[:, :], pm[0:E, :], ACT.Copy).then_inc(f_hot, 1)

            def experts(n):
                for c in range(SLICES):
                    k = SLICES * n + c
                    act.wait_ge(f_z, k + 1)
                    if k >= 2:
                        act.wait_ge(f_o_part, k - 1)
                    nc.scalar.activation(hid[:, k % 2, :], pz[k % 2][:, :], ACT.Relu, bias=b1_t[:, c:c + 1])\
                        .then_inc(f_hid, 1)
                act.wait_ge(f_o_part, SLICES * (n + 1))
                nc.scalar.activation(prod[:, ffn[n], :], po[:, :], ACT.Relu).then_inc(f_ffn_t, 1)

            for i in range(TAIL):
                for what, n in steps_at.get(i, []):
                    if what == "message":
                        message(n)
                    elif what == "flip":
                        flip(n)
                    elif what == "choose":
                        choose(n)
                    elif what == "experts":
                        experts(n)

        @block.vector
        def _(dve):
            links = [0]

            def chain(ins):
                links[0] += 1
                ins.then_inc(dve_chain, 1)
                dve.wait_ge(dve_chain, links[0])

            def layer_norm(k, src, dst, done):
                for b in range(B):
                    ins = nc.vector.bn_stats(stats[:, b, :], src[:, b, :])
                chain(ins)
                for b in range(B):
                    ins = nc.vector.bn_aggr(mv[:, b, :], stats[:, b, :])
                ins.then_inc(norm_var, 1)
                dve.wait_ge(norm_root, k + 1)
                chain(nc.vector.reciprocal(rstd[:, k % 2, :], rstd[:, k % 2, :]))
                for b in range(B):
                    ins = nc.vector.tensor_scalar(dst[:, b, :], src[:, b, :], mv[:, b, 0:1], rstd[:, k % 2, b:b + 1],
                                                  ALU.subtract, ALU.mult)
                ins.then_inc(done, 1)

            def norm_x(s):
                dve.wait_ge(x_in[s % 2], 64 * (s // 2 + 1))
                layer_norm(s, xs[:, s % 2, :, :], xs[:, s % 2, :, :], ln_ready)

            def turn(n):
                for p in pieces_of(n):
                    if slot_free[p] > 0:
                        dve.wait_ge(piece_used, slot_free[p])
                    src = raw[:, n % RAW, :, :].rearrange("p g (b t c) -> p g b t c", b=HB, t=TQ)
                    dst = turned[:, slot_of[p], :, :].rearrange("p b (g r) -> p g b r", r=SQ)
                    nc.vector.transpose(dst, src[:, :, :, p[1] % TQ, :]).then_inc(piece_turned, 1)

            def finish_sums(s):
                dve.wait_ge(sums_root, s + 1)
                chain(nc.vector.reciprocal(rowscale[:, s, :], root[:, :]))
                dve.wait_ge(xw_ready, s + 1)
                nc.vector.tensor_tensor(g[:, s, :, :], pz[1][:, :].rearrange("p (b f) -> p b f", b=B),
                                        rowscale[:, s, :].unsqueeze(2).broadcast_to((P, B, D)),
                                        ALU.mult).then_inc(g_ready, 1)

            norm_x(0)
            for n, (s, q, h) in enumerate(chunks1):
                dve.wait_ge(raw_in[n % RAW], CHUNK_IN * (n // RAW + 1))
                nc.vector.tensor_reduce(part[:, s % 2, ACT_GROUPS:G, 2 * q + h], raw[:, n % RAW, ACT_GROUPS:G, :],
                                        AX.X, ALU.add).then_inc(raw_summed, 1)
                if h == 1 and q == 0:
                    dve.wait_ge(raw_summed, n + 1)
                    dve.wait_ge(raw_by_act, ACT_GROUPS * (n + 1))
                    if s >= 1:
                        dve.wait_ge(sums_full, s)
                    nc.vector.tensor_reduce(part_q[:, :], part[:, s % 2, :, :], AX.X, ALU.add)\
                        .then_inc(sums_part, 1)
                turn(n)
                if h == 1 and q == 0:
                    finish_sums(s)
                if h == 1 and q == QS - 1 and s + 1 < STRIPS:
                    norm_x(s + 1)

            def turn_chunk(n):
                dve.wait_ge(raw_in[n % RAW], CHUNK_IN * (n // RAW + 1))
                turn(n)

            def merge(s):
                dve.wait_ge(piece_used, done_2[s])
                dve.wait_ge(prod_saved, STRIPS)
                nc.vector.tensor_tensor(by_share(prod[:, s, :]), as_read(open_[s % BANKS]),
                                        by_share(prod[:, s, :]), ALU.add).then_inc(prod_saved, 1)

            def message(n):
                k = STRIPS + n
                dve.wait_ge(x_in[k % 2], 64 * (k // 2 + 1))
                dve.wait_ge(f_msg, n + 1)
                chain(nc.vector.tensor_tensor(x1[:, n % 2, :, :], xs[:, k % 2, :, :], x1[:, n % 2, :, :], ALU.add))
                if n >= 1:
                    dve.wait_ge(f_y_turned, n)
                layer_norm(k, x1[:, n % 2, :, :], y, f_y)

            def route(n):
                def wide(v):
                    return v.unsqueeze(2).broadcast_to((P, B, E))
                dve.wait_ge(f_logits, n + 1)
                chain(nc.vector.tensor_tensor(logit[:, :, :], pm[:, 0:B * E].rearrange("p (b e) -> p b e", b=B),
                                              rb[:, :].unsqueeze(1).broadcast_to((P, B, E)), ALU.add))
                chain(nc.vector.tensor_reduce(best[:, :], logit[:, :, :], AX.X, ALU.max))
                chain(nc.vector.tensor_tensor(hit[:, :, :], logit[:, :, :], wide(best[:, :]), ALU.is_equal))
                chain(nc.vector.tensor_tensor(hit[:, :, :], hit[:, :, :], count[:, :, :], ALU.mult))
                chain(nc.vector.tensor_reduce(first[:, :], hit[:, :, :], AX.X, ALU.min))
                if n >= 1:
                    dve.wait_ge(f_hot_turned, n)
                nc.vector.tensor_tensor(onehot[:, :, :], count[:, :, :], wide(first[:, :]), ALU.is_equal)\
                    .then_inc(f_onehot, 1)

            def emit(n):
                dve.wait_ge(f_out_turned, n + 1)
                nc.vector.tensor_tensor(x1[:, n % 2, :, :], pz[0][:, :].rearrange("p (b f) -> p b f", b=B),
                                        x1[:, n % 2, :, :], ALU.add).then_inc(f_res, 1)

            todo = list(range(len(chunks1), len(chunks)))
            for i in range(TAIL):
                while todo and landed[pieces_of(todo[0])[-1]] - N1 < i + LOOK:
                    turn_chunk(todo.pop(0))
                if i < len(phase2) and phase2[i] in closes:
                    merge(phase2[i][0])
                for what, n in steps_at.get(i, []):
                    if what == "message":
                        message(n)
                    elif what == "route":
                        route(n)
                    elif what == "emit":
                        emit(n)

        @block.tensor
        def _(pe):
            pe.wait_ge(const_pool, 11)
            pe.wait_ge(const_dma, 16 * CONST_DMAS)
            nc.tensor.transpose(pm[:, 0:E], rw_nat[:, :], ident[0:E, 0:E])
            nc.tensor.transpose(pm[:, E:E + SLICES], b1_nat[:, :], ident[0:SLICES, 0:SLICES])\
                .then_inc(const_turned, 1)
            pe.wait_ge(const_kept, 1)

            def multiply(p):
                s, t, h = p
                pe.wait_ge(piece_turned, landed[p] + 1)
                if p in opens and place[p] < N1 and s >= BANKS:
                    pe.wait_ge(prod_saved, saved_1[s - BANKS])
                elif p in opens and place[p] >= N1:
                    earlier = [saved_2[r] for r in order2 if r % BANKS == s % BANKS and r > s]
                    pe.wait_ge(prod_saved, max(earlier, default=STRIPS))
                for b in range(HB):
                    ins = nc.tensor.matmul(open_[s % BANKS][:, :], g[:, t, HB * h + b, :],
                                           turned[:, slot_of[p], b, :], start=(b == 0 and p in opens),
                                           stop=(b == HB - 1 and p in closes))
                ins.then_inc(piece_used, 1)

            def turn_ln(s):
                pe.wait_ge(ln_ready, s + 1)
                if s >= 1:
                    pe.wait_ge(ln_t_kept, s)
                for b in range(B):
                    ins = nc.tensor.transpose(pz[0][:, b * P:b * P + P], xs[:, s % 2, b, :], ident[:, :])
                ins.then_inc(ln_turned, 1)

            def times_w(s):
                pe.wait_ge(ln_t_kept, s + 1)
                if s >= 1:
                    pe.wait_ge(g_ready, s)
                for b in range(B):
                    ins = nc.tensor.matmul(pz[1][:, b * D:b * D + D], y_t[:, b * P:b * P + P], w_sb[:, :],
                                           start=True, stop=True)
                ins.then_inc(xw_ready, 1)

            def sum_quads(s):
                pe.wait_ge(sums_part, s + 1)
                if s >= 1:
                    pe.wait_ge(sums_root, s)
                nc.tensor.matmul(po[:, 0:G], quads[:, :, :], part_q[:, :], start=True, stop=True)\
                    .then_inc(sums_full, 1)

            turn_ln(0)
            for s in range(STRIPS):
                late = max(0, len(left[s]) - LATE)
                for p in left[s][:late]:
                    multiply(p)
                times_w(s)
                sum_quads(s)
                for p in left[s][late:]:
                    multiply(p)
                pe.wait_ge(g_ready, s + 1)
                for p in column[s]:
                    multiply(p)
                if s + 1 < STRIPS:
                    turn_ln(s + 1)

            def message(n):
                s = ffn[n]
                pe.wait_ge(prod_saved, saved_2.get(s, STRIPS))
                if n >= 1:
                    pe.wait_ge(f_hot, n)
                for b in range(B):
                    ins = nc.tensor.transpose(pm[:, b * D:b * D + D], prod[:, s, b * P:b * P + P], ident[:, :])
                ins.then_inc(f_prod_turned, 1)

            def flip(n):
                pe.wait_ge(f_y, n + 1)
                pe.wait_ge(f_msg, n + 1)
                for b in range(B):
                    ins = nc.tensor.transpose(pm[:, b * P:b * P + P], y[:, b, :], ident[:, :])
                ins.then_inc(f_y_turned, 1)

            def route(n):
                pe.wait_ge(f_y_t, n + 1)
                for b in range(B):
                    ins = nc.tensor.matmul(pm[:, b * E:b * E + E], y_t[:, b * P:b * P + P], rw_t[:, :],
                                           start=True, stop=True)
                ins.then_inc(f_logits, 1)

            def choose(n):
                pe.wait_ge(f_onehot, n + 1)
                for b in range(B):
                    ins = nc.tensor.transpose(pm[0:E, b * P:b * P + P], onehot[:, b, :], ident[:, :])
                ins.then_inc(f_hot_turned, 1)

            def experts(n):
                pe.wait_ge(f_hot, n + 1)
                if n == 0:
                    pe.wait_ge(experts_in, 32)
                if n >= 1:
                    pe.wait_ge(f_res, n)
                    pe.wait_ge(f_ffn_t, n)

                def hidden(c):
                    k = SLICES * n + c
                    if k >= 2:
                        pe.wait_ge(f_hid, k - 1)
                    nc.tensor.matmul(pz[k % 2][:, :], w1_sb[:, EC * c:EC * c + EC, :], y_t[:, :],
                                     start=True, stop=False)
                    nc.tensor.matmul(pz[k % 2][:, :], off[:, EC * c:EC * c + EC, :], hot_b[:, :],
                                     start=False, stop=True).then_inc(f_z, 1)

                def output(c):
                    k = SLICES * n + c
                    pe.wait_ge(f_hid, k + 1)
                    if c == 0:
                        nc.tensor.matmul(po[:, :], b2_sb[:, :], hot_f[:, :], start=True, stop=False)
                    nc.tensor.matmul(po[:, :], w2_sb[:, c, :], hid[:, k % 2, :], start=False,
                                     stop=(c == SLICES - 1)).then_inc(f_o_part, 1)

                hidden(0)
                for c in range(1, SLICES):
                    hidden(c)
                    output(c - 1)
                output(SLICES - 1)

            def emit(n):
                pe.wait_ge(f_ffn_t, n + 1)
                for b in range(B):
                    ins = nc.tensor.transpose(pz[0][:, b * P:b * P + P], prod[:, ffn[n], b * P:b * P + P], ident[:, :])
                ins.then_inc(f_out_turned, 1)

            for i in range(TAIL):
                if i < len(phase2):
                    multiply(phase2[i])
                for what, n in steps_at.get(i, []):
                    {"message": message, "flip": flip, "route": route, "choose": choose,
                     "experts": experts, "emit": emit}[what](n)


_INS = ["x", "adj", "L0_gnn_W", "L0_ffn_router_w", "L0_ffn_router_b", "L0_ffn_W1", "L0_ffn_b1", "L0_ffn_W2",
        "L0_ffn_b2"]


def kernel(**inputs):
    import numpy as np
    import concourse.bacc as bacc
    from concourse.bass_utils import run_bass_kernel_spmd

    nc = bacc.Bacc("TRN2", target_bir_lowering=False, num_devices=1)
    arrays, args = {}, []
    for name in _INS:
        a = np.ascontiguousarray(inputs[name])
        arrays[f"in_{name}"] = a
        args.append(nc.dram_tensor(f"in_{name}", a.shape, mybir.dt.from_np(a.dtype), kind="ExternalInput").ap())
    shape = arrays["in_x"].shape
    args.append(nc.dram_tensor("out_0", shape, mybir.dt.float32, kind="ExternalOutput").ap())
    gnn_ffn_kernel(nc, *args)
    r = run_bass_kernel_spmd(nc, [arrays], core_ids=[0])
    return r.results[0]["out_0"]
```

```python
from contextlib import ExitStack

import concourse.bass as bass
from concourse import mybir


def gnn_ffn_kernel(nc, x, adj, gnn_w, router_w, router_b, w1, b1, w2, b2, out):
    F32, BF16 = mybir.dt.float32, mybir.dt.bfloat16
    ALU, ACT, AX = mybir.AluOpType, mybir.ActivationFunctionType, mybir.AxisListType

    N, D = x.shape
    E, _, HID = w1.shape
    P = 128
    SQ = 32
    A = B = P // SQ
    G = A * B
    ROWS = G * SQ
    STRIPS = N // ROWS
    TQ = 4
    QS = STRIPS // TQ
    HB = B // 2
    CW = HB * TQ * SQ
    KEEP = [5] + [4] * 4 + [3] * 4 + [2] * 7
    EC = P // HID
    SLICES = E // EC
    EPS = 1e-5

    RAW = 3
    SLOTS = 21
    SLOTS2 = 13
    BANKS1, BANKS2 = 6, 4
    ACT_GROUPS = 11
    LOOK = 10
    LATE = 4

    def kept(s, t):
        return t <= s + KEEP[s]

    chunks1 = [(s, q, h) for s in range(STRIPS) for q in reversed(range(QS)) for h in range(2)]
    order2 = [s for s in reversed(range(STRIPS)) if not kept(s, STRIPS - 1)]
    chunks2 = [(s, q, h) for s in order2 for q in range(QS) if not kept(s, TQ * q + TQ - 1) for h in range(2)]
    chunks = chunks1 + chunks2

    def pieces_of(n):
        s, q, h = chunks[n]
        return [(s, t, h) for t in range(TQ * q, TQ * q + TQ) if kept(s, t) == (n < len(chunks1))]

    turned_order = [p for n in range(len(chunks)) for p in pieces_of(n)]
    landed = {p: i for i, p in enumerate(turned_order)}
    left = {s: [p for p in turned_order if p[0] == s and p[1] < s] for s in range(STRIPS)}
    column = {s: [(r, s, h) for r in range(s + 1) if kept(r, s) for h in range(2)] for s in range(STRIPS)}
    phase1 = [p for s in range(STRIPS) for p in left[s] + column[s]]
    phase2 = turned_order[len(phase1):]
    product = phase1 + phase2
    N1 = len(phase1)
    place = {p: i for i, p in enumerate(product)}
    def ends(part):
        found = {}
        for p in part:
            found[p[0]] = (found.get(p[0], (p,))[0], p)
        return found

    opens = {f for part in (phase1, phase2) for f, _ in ends(part).values()}
    done_1 = {s: place[l] + 1 for s, (_, l) in ends(phase1).items()}
    done_2 = {s: place[l] + 1 for s, (_, l) in ends(phase2).items()}
    closes = {l for part in (phase1, phase2) for _, l in ends(part).values()}
    before = {s: place[(left[s] + column[s])[max(0, len(left[s]) - LATE)]] for s in range(STRIPS)}
    slots = [("turned", k, len(product)) for k in range(SLOTS)]
    slots += [("g", s, before[s]) for s in range(0, STRIPS, 2)]
    slots += [("prod", s, done_1[s]) for s in range(0, STRIPS, 2)]
    slot_of, slot_free = {}, {}
    last = dict.fromkeys(slots, -1)
    for i, p in enumerate(turned_order):
        free = [k for k in slots if place[p] < k[2] and (i < N1 or k[1] < SLOTS2)]
        k = min(free, key=lambda k: (last[k], k[2]))
        slot_of[p], slot_free[p] = k, last[k] + 1
        last[k] = place[p]

    saved_1 = {s: s + 1 for s in range(STRIPS)}
    saved_2 = {s: STRIPS + 1 + i for i, s in enumerate(order2)}

    save_at = {}
    for s in range(STRIPS):
        save_at.setdefault(max(t for t in range(STRIPS) if kept(s, t)) + 1, []).append(s)

    ffn = [s for s in range(STRIPS) if s not in order2] + order2
    start = [(len(phase2) - 1) * n // (STRIPS - 1) for n in range(STRIPS)]
    STEP = (0, 3, 5, 8, 9)
    for n, s in enumerate(ffn):
        assert s not in order2 or start[n] >= done_2[s] - 1 - N1
    steps_at = {}
    QUARTERS = 4
    for n in range(STRIPS):
        if 0 < n < STRIPS:
            steps_at.setdefault(start[n], []).append(("emit", n - 1))
        for k, d in enumerate(STEP[:4]):
            steps_at.setdefault(start[n] + d, []).append((("message", "flip", "route", "choose")[k], n))
        for c in range(QUARTERS):
            steps_at.setdefault(start[n] + STEP[4], []).append(("experts", n, c))
    end = len(phase2) - 1
    assert start[-1] == end and start[-2] + STEP[3] < end
    for i in [i for i in steps_at if i >= start[-2] + STEP[4]]:
        del steps_at[i]
    m, n = STRIPS - 2, STRIPS - 1
    steps_at[end] = [("experts", m, 0), ("message", n), ("experts", m, 1), ("flip", n), ("experts", m, 2),
                     ("route", n), ("experts", m, 3), ("choose", n), ("emit", m)]
    steps_at[end] += [("experts", n, c) for c in range(QUARTERS)] + [("emit", n)]
    steps_at[start[-2] + STEP[0]] = [("emit", m - 1), ("message", m)]
    TAIL = end + 1

    adj_v = adj.rearrange("(q g t r) c -> q t r g c", q=QS, g=G, t=TQ, r=SQ)
    x_v = x.rearrange("(q a b t r) f -> q t a r b f", q=QS, a=A, b=B, t=TQ, r=SQ)
    out_v = out.rearrange("(q a b t r) f -> q t a r b f", q=QS, a=A, b=B, t=TQ, r=SQ)

    ctx = ExitStack()
    with ctx:
        def sb(name, shape, dt=F32):
            return ctx.enter_context(nc.sbuf_tensor(name, shape, dt))

        def sem(name):
            return ctx.enter_context(nc.semaphore(name))

        raw = sb("raw", [P, RAW, G, CW])
        turned = sb("turned", [P, SLOTS, HB, ROWS])
        g = sb("g", [P, STRIPS, B, D])
        prod = sb("prod", [P, STRIPS, ROWS])
        rowscale = sb("rowscale", [P, STRIPS, B])
        root = sb("root", [P, B])
        part = sb("part", [P, 2, G, 2 * QS])
        part_q = sb("part_q", [P, G])
        ident = sb("ident", [P, P])
        quads = sb("quads", [P, A, SQ])
        eps = sb("eps", [P, 1])
        w_sb = sb("w_sb", [P, D])
        rw_nat = sb("rw_nat", [E, D])
        rw_t = sb("rw_t", [P, E])
        rb = sb("rb", [P, E])
        b1_nat = sb("b1_nat", [SLICES, P])
        b1_t = sb("b1_t", [P, SLICES])
        b2_sum = sb("b2_sum", [3 * E, D], BF16)
        xs = sb("xs", [P, 2, B, D])
        stats = sb("stats", [P, B, 6])
        mv = sb("mv", [P, B, 2])
        rstd = sb("rstd", [P, 2, B])
        y_t1 = sb("y_t1", [P, B * P])
        best = sb("best", [P, B])
        first = sb("first", [P, B])
        discard = sb("discard", [P, 2, CW], BF16)

        def spare(k, at, size):
            return turned[:, SLOTS2 + k, :, :].rearrange("p b r -> p (b r)")[:, at:at + size]

        w1_sb = spare(0, 0, E * HID).rearrange("p (e h) -> p e h", e=E)
        w2_sb = spare(1, 0, SLICES * D).rearrange("p (c d) -> p c d", c=SLICES)
        hid = [spare(2, 0, B * P), spare(2, B * P, B * P), spare(6, B * D, B * P)]
        x1 = spare(3, 0, 2 * B * D).rearrange("p (k b d) -> p k b d", k=2, b=B)
        y_t = [y_t1[:, :], spare(4, 0, B * P)]
        y = spare(6, 0, B * D).rearrange("p (b d) -> p b d", b=B)
        hot_t = [spare(5, k * B * P // 2, B * P // 2).bitcast(BF16)[0:3 * E, :] for k in range(2)]
        logit, hit = (spare(4, B * P + k * B * E, B * E).rearrange("p (b e) -> p b e", b=B) for k in range(2))
        b2_sb, b2_rest = (spare(6, B * D + k * D, D)[0:3 * E, :] for k in range(2))
        b2_part = spare(6, B * D + 2 * D, 3 * D // 2).bitcast(BF16)[0:3 * E, :]\
            .rearrange("p (k d) -> p k d", k=3)
        which = spare(7, 0, B * P)
        count = spare(7, B * P, B * E).rearrange("p (b e) -> p b e", b=B)
        ident_b = spare(7, B * P + B * E, P // 2).bitcast(BF16)
        number = spare(7, B * P + B * E + P // 2, P // 2).bitcast(BF16)[0:E, :]
        member = spare(7, B * P + B * E + P, SLICES)
        onehot = spare(5, B * P, 3 * B * E // 2).bitcast(BF16)\
            .rearrange("p (b k e) -> p b k e", b=B, k=3)

        def slot(p):
            kind, k, _ = slot_of[p]
            if kind == "turned":
                return turned[:, k, :, :]
            return prod[:, k:k + HB, :] if kind == "prod" else g[:, k:k + HB, :, :].rearrange("p k b d -> p k (b d)")

        banks = [ctx.enter_context(nc.psum_tensor(f"bank{i}", [P, 512], F32)) for i in range(8)]
        open_1, open_2 = banks[0:4] + banks[6:8], banks[0:4]
        pz = banks[4:6]
        po = banks[6]
        pm = banks[7]

        raw_in = [sem(f"raw_in{i}") for i in range(RAW)]
        raw_summed = sem("raw_summed")
        raw_by_act = sem("raw_by_act")
        piece_turned = sem("piece_turned")
        piece_used = sem("piece_used")
        prod_saved = sem("prod_saved")
        const_pool = sem("const_pool")
        const_dma = sem("const_dma")
        b2_in = sem("b2_in")
        experts_in = sem("experts_in")
        experts_set = sem("experts_set")
        const_turned = sem("const_turned")
        const_kept = sem("const_kept")
        x_in = [sem(f"x_in{i}") for i in range(2)]
        norm_var = sem("norm_var")
        norm_root = sem("norm_root")
        ln_ready = sem("ln_ready")
        sums_part = sem("sums_part")
        sums_full = sem("sums_full")
        sums_root = sem("sums_root")
        g_ready = sem("g_ready")
        dve_chain = sem("dve_chain")
        b2_split = sem("b2_split")
        f_prod_w = sem("f_prod_w")
        f_msg = sem("f_msg")
        f_y = sem("f_y")
        f_y_turned = sem("f_y_turned")
        f_y_t = sem("f_y_t")
        f_logits = sem("f_logits")
        f_onehot = sem("f_onehot")
        f_hot_turned = sem("f_hot_turned")
        f_hot = sem("f_hot")
        f_z = sem("f_z")
        f_which_made = sem("f_which_made")
        f_which = sem("f_which")
        f_relu = sem("f_relu")
        f_hid = sem("f_hid")
        f_o_part = sem("f_o_part")
        f_res = sem("f_res")
        stored = [sem(f"stored{i}") for i in range(2)]

        def as_read(bank):
            return bank[:, :].rearrange("p (a b r) -> p a b r", a=A, b=B)

        def by_share(v):
            return v.rearrange("p (b a r) -> p a b r", a=A, b=B)

        CONST_DMAS = 4
        CHUNK_IN = 16 * A
        block = ctx.enter_context(nc.Block())

        @block.sync
        def _(sp):
            for n, (s, q, h) in enumerate(chunks):
                if n >= RAW:
                    m = n - RAW
                    if pieces_of(m):
                        sp.wait_ge(piece_turned, landed[pieces_of(m)[-1]] + 1)
                    else:
                        sp.wait_ge(raw_summed, m + 1)
                    if m < len(chunks1):
                        sp.wait_ge(raw_by_act, ACT_GROUPS * (m + 1))
                for a in range(A):
                    col = (q * A + a) * 2 * CW + h * CW
                    sp.dma_start(raw[SQ * a:SQ * a + SQ, n % RAW, :, :],
                                 adj_v[s // TQ, s % TQ, :, :, col:col + CW]).then_inc(raw_in[n % RAW], 16)

        @block.gpsimd
        def _(pool):
            pool.memset(ident[:, :], 0.0).then_inc(const_pool, 1)
            pool.memset(quads[:, :, :], 0.0).then_inc(const_pool, 1)
            pool.memset(eps[:, :], EPS).then_inc(const_pool, 1)
            pool.wait_ge(const_pool, 3)
            pool.affine_select(out=ident[:, :], in_=ident[:, :], compare_op=ALU.not_equal, fill=1.0, base=0,
                               pattern=[[-1, P]], channel_multiplier=1).then_inc(const_pool, 1)
            for a in range(A):
                pool.affine_select(out=quads[:, :, :], in_=quads[:, :, :], compare_op=ALU.not_equal, fill=1.0,
                                   base=-SQ * a, pattern=[[0, A], [-1, SQ]], channel_multiplier=1)\
                    .then_inc(const_pool, 1)
                pool.wait_ge(const_pool, 5 + a)

            def load_x(k, s):
                if 2 <= k < STRIPS + 2:
                    pool.wait_ge(g_ready, k - 1)
                elif k >= 2:
                    pool.wait_ge(f_y, k - 1 - STRIPS)
                for a in range(A):
                    pool.dma_start(xs[SQ * a:SQ * a + SQ, k % 2, :, :], x_v[s // TQ, s % TQ, a])\
                        .then_inc(x_in[k % 2], 16)

            for s in range(STRIPS):
                load_x(s, s)
            load_x(STRIPS, ffn[0])
            pool.wait_ge(piece_used, N1)
            for k in range(3):
                pool.dma_start(b2_sb[E * k:E * k + E, :], b2).then_inc(b2_in, 16)
            pool.dma_start(w1_sb, w1.rearrange("e d h -> d e h")).then_inc(experts_in, 16)
            pool.dma_start(w2_sb, w2.rearrange("(c e) h d -> (e h) c d", e=EC)).then_inc(experts_in, 16)
            pool.iota(count, pattern=[[0, B], [1, E]], base=-E, channel_multiplier=0,
                      allow_small_or_imprecise_dtypes=True).then_inc(experts_set, 1)
            pool.tensor_copy(ident_b, ident[:, :]).then_inc(experts_set, 1)
            pool.iota(which[0:E, 0:P], pattern=[[0, P]], base=0, channel_multiplier=1,
                      allow_small_or_imprecise_dtypes=True).then_inc(experts_set, 1)
            for e in range(EC):
                pool.wait_ge(experts_set, 3 + e)
                pool.iota(member[HID * e:HID * e + HID, :], pattern=[[EC, SLICES]], base=e, channel_multiplier=0,
                          allow_small_or_imprecise_dtypes=True).then_inc(experts_set, 1)
            pool.wait_ge(experts_set, 3 + EC)
            pool.tensor_copy(number, which[0:E, 0:P]).then_inc(experts_set, 1)
            for n in range(STRIPS):
                if n + 1 < STRIPS:
                    load_x(STRIPS + n + 1, ffn[n + 1])
                s = ffn[n]
                pool.wait_ge(f_res, n + 1)
                for a in range(A):
                    pool.dma_start(out_v[s // TQ, s % TQ, a], x1[SQ * a:SQ * a + SQ, n % 2, :, :])\
                        .then_inc(stored[n % 2], 16)
            for i in range(2):
                pool.wait_ge(stored[i], STRIPS // 2 * A * 16)

        @block.scalar
        def _(act):
            act.dma_start(w_sb[:, :], gnn_w).then_inc(const_dma, 16)
            act.dma_start(rw_nat[:, :], router_w).then_inc(const_dma, 16)
            act.dma_start(b1_nat[:, :], b1.rearrange("(c e) h -> c (e h)", e=EC)).then_inc(const_dma, 16)
            act.dma_start(rb[:, :], router_b.rearrange("(o e) -> o e", o=1).broadcast_to((P, E)))\
                .then_inc(const_dma, 16)
            act.wait_ge(const_pool, 3)

            def norm_root_(k):
                act.wait_ge(norm_var, k + 1)
                if k >= 2:
                    act.wait_ge(ln_ready if k <= STRIPS else f_y,
                                k - 1 if k <= STRIPS else k - 1 - STRIPS)
                nc.scalar.activation(rstd[:, k % 2, :], mv[:, :, 1], ACT.Sqrt, bias=eps[:, 0:1])\
                    .then_inc(norm_root, 1)

            def save(s):
                act.wait_ge(piece_used, done_1[s])
                nc.scalar.activation(by_share(prod[:, s, :]), as_read(open_1[s % BANKS1]), ACT.Copy).then_inc(prod_saved, 1)

            for n, (s, q, h) in enumerate(chunks1):
                act.wait_ge(raw_in[n % RAW], CHUNK_IN * (n // RAW + 1))
                if h == 0 and q == QS - 1 and s >= 2:
                    act.wait_ge(sums_part, s - 1)
                for i in range(ACT_GROUPS):
                    k = ACT_GROUPS * n + i
                    if k >= 2:
                        act.wait_ge(raw_by_act, k - 1)
                    nc.scalar.activation(discard[:, k % 2, :], raw[:, n % RAW, i, :], ACT.Copy,
                                         accum_out=part[:, s % 2, i, 2 * q + h:2 * q + h + 1])\
                        .then_inc(raw_by_act, 1)
                if n == 0:
                    norm_root_(0)
                if h == 1 and q == 2 and s + 1 < STRIPS:
                    norm_root_(s + 1)
                if n == 2:
                    act.wait_ge(const_turned, 1)
                    nc.scalar.activation(rw_t[:, :], pm[:, 0:E], ACT.Copy)
                    nc.scalar.activation(b1_t[:, :], pm[:, E:E + SLICES], ACT.Copy).then_inc(const_kept, 1)
                if h == 0 and q == 1:
                    for r in save_at.get(s, []):
                        save(r)
                if h == 1 and q == 0:
                    act.wait_ge(sums_full, s + 1)
                    for a in range(A):
                        ins = nc.scalar.activation(root[SQ * a:SQ * a + SQ, :],
                                                   pz[0][SQ * a:SQ * a + SQ, B * a:B * a + B], ACT.Sqrt)
                    ins.then_inc(sums_root, 1)
            for r in save_at[STRIPS]:
                save(r)

            def message(n):
                s = ffn[n]
                act.wait_ge(f_prod_w, n + 1)
                if n >= 2:
                    act.wait_ge(stored[n % 2], n // 2 * A * 16)
                for b in range(B):
                    ins = nc.scalar.activation(x1[:, n % 2, b, :], pm[:, b * D:b * D + D], ACT.Relu,
                                               scale=rowscale[:, s, b:b + 1])
                ins.then_inc(f_msg, 1)
                norm_root_(STRIPS + n)

            def flip(n):
                act.wait_ge(f_y_turned, n + 1)
                nc.scalar.activation(y_t[n % 2], pm[:, :], ACT.Copy).then_inc(f_y_t, 1)

            def choose(n):
                act.wait_ge(f_hot_turned, n + 1)
                nc.scalar.activation(hot_t[n % 2], pm[0:3 * E, :], ACT.Copy).then_inc(f_hot, 1)

            def experts(n, quarter):
                if quarter == 0:
                    act.wait_ge(f_which_made, n + 1)
                    if n >= 1:
                        act.wait_ge(f_hid, SLICES * n)
                    nc.scalar.activation(which, pm[:, :], ACT.Copy).then_inc(f_which, 1)
                for c in range(2 * quarter, 2 * quarter + 2):
                    k = SLICES * n + c
                    act.wait_ge(f_z, k + 1)
                    if k >= 3:
                        act.wait_ge(f_o_part, k - 2)
                    nc.scalar.activation(hid[k % 3], pz[(c + 1) % 2][:, :], ACT.Relu, bias=b1_t[:, c:c + 1])\
                        .then_inc(f_relu, 1)

            for i in range(TAIL):
                for what, *n in steps_at.get(i, []):
                    if what == "message":
                        message(*n)
                    elif what == "flip":
                        flip(*n)
                    elif what == "choose":
                        choose(*n)
                    elif what == "experts":
                        experts(*n)

        @block.vector
        def _(dve):
            links = [0]

            def chain(ins):
                links[0] += 1
                ins.then_inc(dve_chain, 1)
                dve.wait_ge(dve_chain, links[0])

            def layer_norm(k, src, dst, done):
                for b in range(B):
                    ins = nc.vector.bn_stats(stats[:, b, :], src[:, b, :])
                chain(ins)
                for b in range(B):
                    ins = nc.vector.bn_aggr(mv[:, b, :], stats[:, b, :])
                ins.then_inc(norm_var, 1)
                dve.wait_ge(norm_root, k + 1)
                chain(nc.vector.reciprocal(rstd[:, k % 2, :], rstd[:, k % 2, :]))
                for b in range(B):
                    ins = nc.vector.tensor_scalar(dst[:, b, :], src[:, b, :], mv[:, b, 0:1], rstd[:, k % 2, b:b + 1],
                                                  ALU.subtract, ALU.mult)
                ins.then_inc(done, 1)

            def norm_x(s):
                dve.wait_ge(x_in[s % 2], 64 * (s // 2 + 1))
                layer_norm(s, xs[:, s % 2, :, :], xs[:, s % 2, :, :], ln_ready)

            def turn(n):
                for p in pieces_of(n):
                    if slot_free[p] > 0:
                        dve.wait_ge(piece_used, slot_free[p])
                    src = raw[:, n % RAW, :, :].rearrange("p g (b t c) -> p g b t c", b=HB, t=TQ)
                    dst = slot(p).rearrange("p b (g r) -> p g b r", r=SQ)
                    nc.vector.transpose(dst, src[:, :, :, p[1] % TQ, :]).then_inc(piece_turned, 1)

            def finish_sums(s):
                dve.wait_ge(sums_root, s + 1)
                chain(nc.vector.reciprocal(rowscale[:, s, :], root[:, :]))
                dve.wait_ge(ln_ready, s + 1)
                nc.vector.tensor_tensor(g[:, s, :, :], xs[:, s % 2, :, :],
                                        rowscale[:, s, :].unsqueeze(2).broadcast_to((P, B, D)),
                                        ALU.mult).then_inc(g_ready, 1)

            def split_b2():
                dve.wait_ge(b2_in, 16 * 3)
                chain(nc.vector.tensor_copy(b2_part[:, 0, :], b2_sb[:, :]))
                chain(nc.vector.tensor_tensor(b2_rest[:, :], b2_sb[:, :], b2_part[:, 0, :], ALU.subtract))
                chain(nc.vector.tensor_copy(b2_part[:, 1, :], b2_rest[:, :]))
                chain(nc.vector.tensor_tensor(b2_rest[:, :], b2_rest[:, :], b2_part[:, 1, :], ALU.subtract))
                chain(nc.vector.tensor_copy(b2_part[:, 2, :], b2_rest[:, :]))
                for k in range(3):
                    ins = nc.vector.tensor_copy(b2_sum[E * k:E * k + E, :], b2_part[E * k:E * k + E, k, :])
                ins.then_inc(b2_split, 1)

            for n, (s, q, h) in enumerate(chunks1):
                dve.wait_ge(raw_in[n % RAW], CHUNK_IN * (n // RAW + 1))
                nc.vector.tensor_reduce(part[:, s % 2, ACT_GROUPS:G, 2 * q + h], raw[:, n % RAW, ACT_GROUPS:G, :],
                                        AX.X, ALU.add).then_inc(raw_summed, 1)
                if h == 1 and q == 0:
                    dve.wait_ge(raw_summed, n + 1)
                    dve.wait_ge(raw_by_act, ACT_GROUPS * (n + 1))
                    if s >= 1:
                        dve.wait_ge(sums_full, s)
                    nc.vector.tensor_reduce(part_q[:, :], part[:, s % 2, :, :], AX.X, ALU.add)\
                        .then_inc(sums_part, 1)
                turn(n)
                if h == 1 and q == 0:
                    finish_sums(s)
                if n == 0:
                    norm_x(0)
                if h == 1 and q == 2 and s + 1 < STRIPS:
                    norm_x(s + 1)

            def turn_chunk(n):
                dve.wait_ge(raw_in[n % RAW], CHUNK_IN * (n // RAW + 1))
                turn(n)

            def merge(s):
                dve.wait_ge(piece_used, done_2[s])
                dve.wait_ge(prod_saved, STRIPS)
                nc.vector.tensor_tensor(by_share(prod[:, s, :]), as_read(open_2[s % BANKS2]),
                                        by_share(prod[:, s, :]), ALU.add).then_inc(prod_saved, 1)

            def message(n):
                k = STRIPS + n
                dve.wait_ge(x_in[k % 2], 64 * (k // 2 + 1))
                dve.wait_ge(f_msg, n + 1)
                chain(nc.vector.tensor_tensor(x1[:, n % 2, :, :], xs[:, k % 2, :, :], x1[:, n % 2, :, :], ALU.add))
                if n >= 1:
                    dve.wait_ge(f_y_turned, n)
                layer_norm(k, x1[:, n % 2, :, :], y, f_y)

            def route(n):
                def wide(v):
                    return v.unsqueeze(2).broadcast_to((P, B, E))
                if n == 0:
                    dve.wait_ge(experts_set, 4 + EC)
                dve.wait_ge(f_logits, n + 1)
                chain(nc.vector.tensor_tensor(logit[:, :, :], pm[:, 0:B * E].rearrange("p (b e) -> p b e", b=B),
                                              rb[:, :].unsqueeze(1).broadcast_to((P, B, E)), ALU.add))
                chain(nc.vector.tensor_reduce(best[:, :], logit[:, :, :], AX.X, ALU.max))
                chain(nc.vector.tensor_tensor(hit[:, :, :], logit[:, :, :], wide(best[:, :]), ALU.is_equal))
                chain(nc.vector.tensor_tensor(hit[:, :, :], hit[:, :, :], count[:, :, :], ALU.mult))
                chain(nc.vector.tensor_reduce(first[:, :], hit[:, :, :], AX.X, ALU.min))
                if n >= 1:
                    dve.wait_ge(f_hot_turned, n)
                nc.vector.tensor_tensor(onehot, count[:, :, :].unsqueeze(2).broadcast_to((P, B, 3, E)),
                                        first[:, :].unsqueeze(2).unsqueeze(3).broadcast_to((P, B, 3, E)),
                                        ALU.is_equal)\
                    .then_inc(f_onehot, 1)

            def experts(n, quarter):
                dve.wait_ge(f_which, n + 1)
                for c in range(2 * quarter, 2 * quarter + 2):
                    k = SLICES * n + c
                    dve.wait_ge(f_relu, k + 1)
                    nc.vector.scalar_tensor_tensor(hid[k % 3], which, member[:, c:c + 1], hid[k % 3],
                                                   ALU.is_equal, ALU.mult).then_inc(f_hid, 1)

            def emit(n):
                dve.wait_ge(f_o_part, SLICES * (n + 1))
                nc.vector.scalar_tensor_tensor(x1[:, n % 2, :, :], po[:, :].rearrange("p (b f) -> p b f", b=B), 0.0,
                                               x1[:, n % 2, :, :], ALU.max, ALU.add).then_inc(f_res, 1)

            todo = list(range(len(chunks1), len(chunks)))
            for i in range(TAIL):
                while todo and landed[pieces_of(todo[0])[-1]] - N1 < i + LOOK:
                    turn_chunk(todo.pop(0))
                if i == STEP[1]:
                    split_b2()
                if i < len(phase2) and phase2[i] in closes:
                    merge(phase2[i][0])
                for what, *n in steps_at.get(i, []):
                    if what == "message":
                        message(*n)
                    elif what == "route":
                        route(*n)
                    elif what == "experts":
                        experts(*n)
                    elif what == "emit":
                        emit(*n)

        @block.tensor
        def _(pe):
            pe.wait_ge(const_pool, 8)
            pe.wait_ge(const_dma, 16 * CONST_DMAS)
            nc.tensor.transpose(pm[:, 0:E], rw_nat[:, :], ident[0:E, 0:E])
            nc.tensor.transpose(pm[:, E:E + SLICES], b1_nat[:, :], ident[0:SLICES, 0:SLICES])\
                .then_inc(const_turned, 1)
            def multiply(p):
                s, t, h = p
                pe.wait_ge(piece_turned, landed[p] + 1)
                if place[p] < N1:
                    bank = open_1[s % BANKS1]
                    if p in opens and s == BANKS1 - 1:
                        pe.wait_ge(const_kept, 1)
                    if p in opens and s >= BANKS1:
                        pe.wait_ge(prod_saved, saved_1[s - BANKS1])
                else:
                    bank = open_2[s % BANKS2]
                    if p in opens:
                        earlier = [saved_2[r] for r in order2 if r % BANKS2 == s % BANKS2 and r > s]
                        pe.wait_ge(prod_saved, max(earlier, default=STRIPS))
                for b in range(HB):
                    ins = nc.tensor.matmul(bank[:, :], g[:, t, HB * h + b, :], slot(p)[:, b, :],
                                           start=(b == 0 and p in opens), stop=(b == HB - 1 and p in closes))
                ins.then_inc(piece_used, 1)

            def sum_quads(s):
                pe.wait_ge(sums_part, s + 1)
                if s >= 1:
                    pe.wait_ge(sums_root, s)
                nc.tensor.matmul(pz[0][:, 0:G], quads[:, :, :], part_q[:, :], start=True, stop=True)\
                    .then_inc(sums_full, 1)

            for s in range(STRIPS):
                late = max(0, len(left[s]) - LATE)
                for p in left[s][:late]:
                    multiply(p)
                sum_quads(s)
                for p in left[s][late:]:
                    multiply(p)
                pe.wait_ge(g_ready, s + 1)
                for p in column[s]:
                    multiply(p)

            def message(n):
                s = ffn[n]
                pe.wait_ge(prod_saved, saved_2.get(s, STRIPS))
                if n >= 1:
                    pe.wait_ge(f_which, n)
                for b in range(B):
                    ins = nc.tensor.matmul(pm[:, b * D:b * D + D], prod[:, s, b * P:b * P + P], w_sb[:, :],
                                           start=True, stop=True)
                ins.then_inc(f_prod_w, 1)

            def flip(n):
                pe.wait_ge(f_y, n + 1)
                pe.wait_ge(f_msg, n + 1)
                for b in range(B):
                    ins = nc.tensor.transpose(pm[:, b * P:b * P + P], y[:, b, :], ident[:, :])
                ins.then_inc(f_y_turned, 1)

            def route(n):
                pe.wait_ge(f_y_t, n + 1)
                for b in range(B):
                    ins = nc.tensor.matmul(pm[:, b * E:b * E + E], y_t[n % 2][:, b * P:b * P + P], rw_t[:, :],
                                           start=True, stop=True)
                ins.then_inc(f_logits, 1)

            def choose(n):
                pe.wait_ge(f_onehot, n + 1)
                for b in range(B):
                    ins = nc.tensor.matmul(pm[0:3 * E, b * P:b * P + P], onehot[:, b, :, :], ident_b,
                                           start=True, stop=True)
                ins.then_inc(f_hot_turned, 1)

            def experts(n, quarter):
                def hidden(c):
                    k = SLICES * n + c
                    if k == 0:
                        pe.wait_ge(experts_in, 32)
                    if k >= 2:
                        pe.wait_ge(f_relu, k - 1)
                    bank = pz[(c + 1) % 2]
                    nc.tensor.matmul(bank[:, :], w1_sb[:, EC * c:EC * c + EC, :], y_t[n % 2],
                                     start=True, stop=True).then_inc(f_z, 1)

                def output(c):
                    k = SLICES * n + c
                    if c == 0:
                        if n == 0:
                            pe.wait_ge(b2_split, 1)
                        else:
                            pe.wait_ge(f_res, n)
                        for b in range(B):
                            nc.tensor.matmul(po[:, b * D:b * D + D], hot_t[n % 2][:, b * P:b * P + P], b2_sum[:, :],
                                             start=(b == 0), stop=False, skip_group_check=True)
                    pe.wait_ge(f_hid, k + 1)
                    for b in range(B):
                        ins = nc.tensor.matmul(po[:, b * D:b * D + D], hid[k % 3][:, b * P:b * P + P], w2_sb[:, c, :],
                                               start=False, stop=(c == SLICES - 1 and b == B - 1),
                                               skip_group_check=True)
                    ins.then_inc(f_o_part, 1)

                if quarter == 0:
                    if n == 0:
                        pe.wait_ge(experts_set, 4 + EC)
                    pe.wait_ge(f_hot, n + 1)
                    nc.tensor.matmul(pm[:, :], number, hot_t[n % 2][0:E, :], start=True, stop=True)\
                        .then_inc(f_which_made, 1)
                for c in range(2 * quarter, 2 * quarter + 2):
                    hidden(c)
                    if c > 1:
                        output(c - 2)
                if quarter == QUARTERS - 1:
                    output(SLICES - 2)
                    output(SLICES - 1)

            for i in range(TAIL):
                if i < len(phase2):
                    multiply(phase2[i])
                for what, *n in steps_at.get(i, []):
                    if what == "message":
                        message(*n)
                    elif what == "flip":
                        flip(*n)
                    elif what == "route":
                        route(*n)
                    elif what == "choose":
                        choose(*n)
                    elif what == "experts":
                        experts(*n)


_INS = ["x", "adj", "L0_gnn_W", "L0_ffn_router_w", "L0_ffn_router_b", "L0_ffn_W1", "L0_ffn_b1", "L0_ffn_W2",
        "L0_ffn_b2"]


def kernel(**inputs):
    import numpy as np
    import concourse.bacc as bacc
    from concourse.bass_utils import run_bass_kernel_spmd

    nc = bacc.Bacc("TRN2", target_bir_lowering=False, num_devices=1)
    arrays, args = {}, []
    for name in _INS:
        a = np.ascontiguousarray(inputs[name])
        arrays[f"in_{name}"] = a
        args.append(nc.dram_tensor(f"in_{name}", a.shape, mybir.dt.from_np(a.dtype), kind="ExternalInput").ap())
    shape = arrays["in_x"].shape
    args.append(nc.dram_tensor("out_0", shape, mybir.dt.float32, kind="ExternalOutput").ap())
    gnn_ffn_kernel(nc, *args)
    r = run_bass_kernel_spmd(nc, [arrays], core_ids=[0])
    return r.results[0]["out_0"]
```
